# Optimizing a Trainium2 kernel written in Bass

```python
import numpy as np
import jax
import jax.numpy as jnp

def _softmax(x, axis=-1):
    return jax.nn.softmax(x, axis=axis)

def _gelu(x):
    return jax.nn.gelu(x, approximate=True)

def _silu(x):
    return jax.nn.silu(x)

def _sigmoid(x):
    return jax.nn.sigmoid(x)

def _layernorm(x, axis=-1, eps=1e-05):
    m = jnp.mean(x, axis=axis, keepdims=True)
    v = jnp.var(x, axis=axis, keepdims=True)
    return (x - m) / jnp.sqrt(v + eps)

def _scatter_add(tgt, idx, src, axis=0):
    return tgt.at[idx].add(src)

def _segment_sum(src, seg, n):
    return jax.ops.segment_sum(src, seg, n)
kernel_name = 'mk_vit_tower_cls_d2_tok_img768_r4_66144b'

def setup_inputs(seed: int=0):
    np.random.seed(seed)
    _w = jnp.asarray

    def _rec_inputs():
        import jax
        import jax.numpy as jnp
        _rk = jax.random.key(seed)
        x = -0.00016672 + 0.999947 * jax.random.normal(jax.random.fold_in(_rk, 1), (32, 3, 64, 64), jnp.float32)
        cls_tok = 0.02 * jax.random.normal(jax.random.fold_in(_rk, 5), (1, 1, 192), jnp.float32)
        return (x, cls_tok)
    x, cls_tok = _rec_inputs()

    def _L0_tok_setup():
        import jax, jax.numpy as jnp
        import numpy as np
        PATCH = 16

        def _unfold_patches(x):
            B, C, H, W = x.shape
            gh, gw = (H // PATCH, W // PATCH)
            x = x.reshape(B, C, gh, PATCH, gw, PATCH)
            x = x.transpose(0, 2, 4, 1, 3, 5)
            return x.reshape(B, gh * gw, C * PATCH * PATCH)
        key = jax.random.key(seed)
        k1, k2, k3 = jax.random.split(key, 3)
        x = jax.random.normal(k1, (64, 3, 96, 96), dtype=jnp.float32)
        in_feat = 3 * PATCH * PATCH
        W = jax.random.normal(k2, (192, in_feat), dtype=jnp.float32) * (1.0 / np.sqrt(in_feat))
        b = jax.random.normal(k3, (192,), dtype=jnp.float32) * 0.01
        return {'x': x, 'W': W, 'b': b}
    _L0_tok_all = _L0_tok_setup()
    _L0_tok_in = {k: v for k, v in _L0_tok_all.items() if k in ('W', 'b')}
    del _L0_tok_all

    def _L0_attn_setup():
        import jax, jax.numpy as jnp
        import numpy as np
        B, N, C, H = (8, 256, 192, 12)
        D = C // H
        SCALE = D ** (-0.5)
        key = jax.random.key(seed)
        ks = jax.random.split(key, 5)
        s = lambda k, sh, fan: jax.random.normal(k, sh, jnp.float32) * fan ** (-0.5)
        return {'x': jax.random.normal(ks[0], (B, N, C), jnp.float32), 'w_qkv': s(ks[1], (C, 3 * C), C), 'b_qkv': jnp.zeros((3 * C,), jnp.float32), 'w_l': s(ks[2], (H, H), H), 'b_l': jnp.zeros((H,), jnp.float32), 'w_w': s(ks[3], (H, H), H), 'b_w': jnp.zeros((H,), jnp.float32), 'w_proj': s(ks[4], (C, C), C), 'b_proj': jnp.zeros((C,), jnp.float32)}
    _L0_attn_all = _L0_attn_setup()
    _L0_attn_in = {k: v for k, v in _L0_attn_all.items() if k in ('w_qkv', 'b_qkv', 'w_l', 'b_l', 'w_w', 'b_w', 'w_proj', 'b_proj')}
    del _L0_attn_all

    def _L0_ffn_setup():
        import jax, jax.numpy as jnp
        import numpy as np
        E = 16
        K = 4
        H = 192
        I = 384
        LIMIT = 7.0
        ALPHA = 1.702
        EPS = 1e-05

        def rmsnorm(x, scale):
            xf = x.astype(jnp.float32)
            inv = jax.lax.rsqrt(jnp.mean(xf * xf, axis=-1, keepdims=True) + EPS)
            return (xf * inv).astype(x.dtype) * scale

        def swiglu(x, limit=LIMIT, alpha=ALPHA):
            x_glu = x[..., ::2]
            x_lin = x[..., 1::2]
            x_glu = jnp.minimum(x_glu, limit)
            x_lin = jnp.clip(x_lin, -limit, limit)
            return x_glu * jax.nn.sigmoid(alpha * x_glu) * (x_lin + 1.0)
        key = jax.random.key(seed)
        ks = jax.random.split(key, 7)
        s = 0.02
        return {'x': jax.random.normal(ks[0], (2, 256, H), dtype=jnp.float32), 'norm_scale': jnp.ones((H,), dtype=jnp.float32), 'gate_w': jax.random.normal(ks[1], (E, H), dtype=jnp.float32) * s, 'gate_b': jnp.zeros((E,), dtype=jnp.float32), 'mlp1_w': jax.random.normal(ks[2], (E, 2 * I, H), dtype=jnp.float32) * s, 'mlp1_b': jax.random.normal(ks[3], (E, 2 * I), dtype=jnp.float32) * s, 'mlp2_w': jax.random.normal(ks[4], (E, H, I), dtype=jnp.float32) * s, 'mlp2_b': jax.random.normal(ks[5], (E, H), dtype=jnp.float32) * s}
    _L0_ffn_all = _L0_ffn_setup()
    _L0_ffn_in = {k: v for k, v in _L0_ffn_all.items() if k in ('norm_scale', 'gate_w', 'gate_b', 'mlp1_w', 'mlp1_b', 'mlp2_w', 'mlp2_b')}
    del _L0_ffn_all

    def _L1_attn_setup():
        import jax, jax.numpy as jnp
        import numpy as np
        B, S, D = (8, 1024, 192)
        NB = D // 3

        def _quat_rotate(h_blocks, biv):
            norm_b = jnp.maximum(jnp.linalg.norm(biv, axis=-1, keepdims=True), 1e-08)
            half = norm_b * 0.5
            w = jnp.cos(half)[..., 0]
            s = (jnp.sin(half) / norm_b)[..., 0]
            qx = s * biv[..., 2]
            qy = -s * biv[..., 1]
            qz = s * biv[..., 0]
            vx, vy, vz = (h_blocks[..., 0], h_blocks[..., 1], h_blocks[..., 2])
            tx = 2.0 * (qy * vz - qz * vy)
            ty = 2.0 * (qz * vx - qx * vz)
            tz = 2.0 * (qx * vy - qy * vx)
            rx = vx + w * tx + (qy * tz - qz * ty)
            ry = vy + w * ty + (qz * tx - qx * tz)
            rz = vz + w * tz + (qx * ty - qy * tx)
            return jnp.stack([rx, ry, rz], axis=-1)
        key = jax.random.key(seed)
        ks = jax.random.split(key, 6)
        x = jax.random.normal(ks[0], (B, S, D), jnp.float32)
        Wb = jax.random.normal(ks[1], (D, NB * 3), jnp.float32) * 0.02
        bb = jnp.zeros((NB * 3,), jnp.float32)
        Wd = jax.random.normal(ks[2], (D, 1), jnp.float32) * 0.02
        bd = jnp.full((1,), 1.4, jnp.float32)
        Wi = jax.random.normal(ks[3], (D, D), jnp.float32) * 0.02
        bi = jax.random.normal(ks[4], (D,), jnp.float32) * 0.02
        gamma = jnp.ones((D,), jnp.float32)
        beta = jnp.zeros((D,), jnp.float32)
        return dict(x=x, Wb=Wb, bb=bb, Wd=Wd, bd=bd, Wi=Wi, bi=bi, gamma=gamma, beta=beta)
    _L1_attn_all = _L1_attn_setup()
    _L1_attn_in = {k: v for k, v in _L1_attn_all.items() if k in ('Wb', 'bb', 'Wd', 'bd', 'Wi', 'bi', 'gamma', 'beta')}
    del _L1_attn_all

    def _L1_ffn_setup():
        import jax, jax.numpy as jnp
        import numpy as np
        D_MODEL = 192
        D_FF = 768
        NUM_EXPERTS = 8
        EXPERT_CAPACITY = 256
        key = jax.random.key(seed)
        k0, k1, k2, k3 = jax.random.split(key, 4)
        hidden_states = jax.random.normal(k0, (2, 256, D_MODEL), dtype=jnp.float32)
        router_w = jax.random.normal(k1, (D_MODEL, NUM_EXPERTS), dtype=jnp.float32) * D_MODEL ** (-0.5)
        wi = jax.random.normal(k2, (NUM_EXPERTS, D_MODEL, D_FF), dtype=jnp.float32) * D_MODEL ** (-0.5)
        wo = jax.random.normal(k3, (NUM_EXPERTS, D_FF, D_MODEL), dtype=jnp.float32) * D_FF ** (-0.5)
        return {'hidden_states': hidden_states, 'router_w': router_w, 'wi': wi, 'wo': wo}
    _L1_ffn_all = _L1_ffn_setup()
    _L1_ffn_in = {k: v for k, v in _L1_ffn_all.items() if k in ('router_w', 'wi', 'wo')}
    del _L1_ffn_all
    return {'x': x, 'cls_tok': cls_tok, 'L0_tok_W': _L0_tok_in['W'], 'L0_tok_b': _L0_tok_in['b'], 'L0_attn_w_qkv': _L0_attn_in['w_qkv'], 'L0_attn_b_qkv': _L0_attn_in['b_qkv'], 'L0_attn_w_l': _L0_attn_in['w_l'], 'L0_attn_b_l': _L0_attn_in['b_l'], 'L0_attn_w_w': _L0_attn_in['w_w'], 'L0_attn_b_w': _L0_attn_in['b_w'], 'L0_attn_w_proj': _L0_attn_in['w_proj'], 'L0_attn_b_proj': _L0_attn_in['b_proj'], 'L0_ffn_norm_scale': _L0_ffn_in['norm_scale'], 'L0_ffn_gate_w': _L0_ffn_in['gate_w'], 'L0_ffn_gate_b': _L0_ffn_in['gate_b'], 'L0_ffn_mlp1_w': _L0_ffn_in['mlp1_w'], 'L0_ffn_mlp1_b': _L0_ffn_in['mlp1_b'], 'L0_ffn_mlp2_w': _L0_ffn_in['mlp2_w'], 'L0_ffn_mlp2_b': _L0_ffn_in['mlp2_b'], 'L1_attn_Wb': _L1_attn_in['Wb'], 'L1_attn_bb': _L1_attn_in['bb'], 'L1_attn_Wd': _L1_attn_in['Wd'], 'L1_attn_bd': _L1_attn_in['bd'], 'L1_attn_Wi': _L1_attn_in['Wi'], 'L1_attn_bi': _L1_attn_in['bi'], 'L1_attn_gamma': _L1_attn_in['gamma'], 'L1_attn_beta': _L1_attn_in['beta'], 'L1_ffn_router_w': _L1_ffn_in['router_w'], 'L1_ffn_wi': _L1_ffn_in['wi'], 'L1_ffn_wo': _L1_ffn_in['wo']}

def reference(x, cls_tok, L0_tok_W, L0_tok_b, L0_attn_w_qkv, L0_attn_b_qkv, L0_attn_w_l, L0_attn_b_l, L0_attn_w_w, L0_attn_b_w, L0_attn_w_proj, L0_attn_b_proj, L0_ffn_norm_scale, L0_ffn_gate_w, L0_ffn_gate_b, L0_ffn_mlp1_w, L0_ffn_mlp1_b, L0_ffn_mlp2_w, L0_ffn_mlp2_b, L1_attn_Wb, L1_attn_bb, L1_attn_Wd, L1_attn_bd, L1_attn_Wi, L1_attn_bi, L1_attn_gamma, L1_attn_beta, L1_ffn_router_w, L1_ffn_wi, L1_ffn_wo):
    import jax
    import jax.numpy as jnp

    def _L0_tok_ref(x, W, b):
        import jax, jax.numpy as jnp
        import numpy as np
        PATCH = 16

        def _unfold_patches(x):
            B, C, H, W = x.shape
            gh, gw = (H // PATCH, W // PATCH)
            x = x.reshape(B, C, gh, PATCH, gw, PATCH)
            x = x.transpose(0, 2, 4, 1, 3, 5)
            return x.reshape(B, gh * gw, C * PATCH * PATCH)
        patches = _unfold_patches(x)
        return jnp.einsum('blk,ek->ble', patches, W) + b

    def _L0_attn_ref(x, w_qkv, b_qkv, w_l, b_l, w_w, b_w, w_proj, b_proj):
        import jax, jax.numpy as jnp
        import numpy as np
        B, N, C, H = (8, 256, 192, 12)
        D = C // H
        SCALE = D ** (-0.5)
        Bq, Nq, Cq = x.shape
        qkv = (x @ w_qkv + b_qkv).reshape(Bq, Nq, 3, H, D).transpose(2, 0, 3, 1, 4)
        q, k, v = (qkv[0] * SCALE, qkv[1], qkv[2])
        attn = jnp.einsum('bhnd,bhmd->bhnm', q, k)
        attn = jnp.einsum('bhnm,hg->bgnm', attn, w_l) + b_l[None, :, None, None]
        attn = jax.nn.softmax(attn, axis=-1)
        attn = jnp.einsum('bhnm,hg->bgnm', attn, w_w) + b_w[None, :, None, None]
        out = jnp.einsum('bhnm,bhmd->bnhd', attn, v).reshape(Bq, Nq, Cq)
        return out @ w_proj + b_proj

    def _L0_ffn_ref(x, norm_scale, gate_w, gate_b, mlp1_w, mlp1_b, mlp2_w, mlp2_b):
        import jax, jax.numpy as jnp
        import numpy as np
        E = 16
        K = 4
        H = 192
        I = 384
        LIMIT = 7.0
        ALPHA = 1.702
        EPS = 1e-05

        def rmsnorm(x, scale):
            xf = x.astype(jnp.float32)
            inv = jax.lax.rsqrt(jnp.mean(xf * xf, axis=-1, keepdims=True) + EPS)
            return (xf * inv).astype(x.dtype) * scale

        def swiglu(x, limit=LIMIT, alpha=ALPHA):
            x_glu = x[..., ::2]
            x_lin = x[..., 1::2]
            x_glu = jnp.minimum(x_glu, limit)
            x_lin = jnp.clip(x_lin, -limit, limit)
            return x_glu * jax.nn.sigmoid(alpha * x_glu) * (x_lin + 1.0)
        B, T, _ = x.shape
        t = rmsnorm(x, norm_scale)
        g = jnp.einsum('bth,eh->bte', t, gate_w) + gate_b
        top_vals, top_idx = jax.lax.top_k(g, K)
        route_w = jax.nn.softmax(top_vals, axis=-1)
        t_flat = t.reshape(B * T, H)
        idx_flat = top_idx.reshape(B * T, K)
        w_flat = route_w.reshape(B * T, K)
        onehot = jax.nn.one_hot(idx_flat, E, dtype=t_flat.dtype)
        comb = jnp.einsum('nke,nk->ne', onehot, w_flat)
        h = jnp.einsum('nh,ech->nec', t_flat, mlp1_w) + mlp1_b
        a = swiglu(h)
        y = jnp.einsum('nec,ehc->neh', a, mlp2_w) + mlp2_b
        out_flat = jnp.einsum('neh,ne->nh', y, comb)
        return x + out_flat.reshape(B, T, H)

    def _L1_attn_ref(x, Wb, bb, Wd, bd, Wi, bi, gamma, beta):
        import jax, jax.numpy as jnp
        import numpy as np
        B, S, D = (8, 1024, 192)
        NB = D // 3

        def _quat_rotate(h_blocks, biv):
            norm_b = jnp.maximum(jnp.linalg.norm(biv, axis=-1, keepdims=True), 1e-08)
            half = norm_b * 0.5
            w = jnp.cos(half)[..., 0]
            s = (jnp.sin(half) / norm_b)[..., 0]
            qx = s * biv[..., 2]
            qy = -s * biv[..., 1]
            qz = s * biv[..., 0]
            vx, vy, vz = (h_blocks[..., 0], h_blocks[..., 1], h_blocks[..., 2])
            tx = 2.0 * (qy * vz - qz * vy)
            ty = 2.0 * (qz * vx - qx * vz)
            tz = 2.0 * (qx * vy - qy * vx)
            rx = vx + w * tx + (qy * tz - qz * ty)
            ry = vy + w * ty + (qz * tx - qx * tz)
            rz = vz + w * tz + (qx * ty - qy * tx)
            return jnp.stack([rx, ry, rz], axis=-1)
        b, s, d = x.shape
        nb = d // 3
        biv = (x @ Wb + bb).reshape(b, s, nb, 3)
        dec = jax.nn.sigmoid(x @ Wd + bd)
        inj = x @ Wi + bi
        biv_t = jnp.swapaxes(biv, 0, 1)
        dec_t = jnp.swapaxes(dec, 0, 1)
        inj_t = jnp.swapaxes(inj, 0, 1)
        h0 = jnp.zeros((b, d), x.dtype)

        def step(h, ins):
            bv, dc, ij = ins
            rot = _quat_rotate(h.reshape(b, nb, 3), bv).reshape(b, d)
            h_next = dc * rot + ij
            return (h_next, h_next)
        _, hs = jax.lax.scan(step, h0, (biv_t, dec_t, inj_t))
        hs = jnp.swapaxes(hs, 0, 1)
        mu = jnp.mean(hs, axis=-1, keepdims=True)
        var = jnp.var(hs, axis=-1, keepdims=True)
        y = (hs - mu) / jnp.sqrt(var + 1e-05) * gamma + beta
        return y + x

    def _L1_ffn_ref(hidden_states, router_w, wi, wo):
        import jax, jax.numpy as jnp
        import numpy as np
        D_MODEL = 192
        D_FF = 768
        NUM_EXPERTS = 8
        EXPERT_CAPACITY = 256
        B, S, d = hidden_states.shape
        E = router_w.shape[1]
        x = hidden_states.reshape(-1, d)
        logits = x.astype(jnp.float32) @ router_w.astype(jnp.float32)
        probs = jax.nn.softmax(logits, axis=-1).astype(x.dtype)
        p = jnp.max(probs, axis=-1)
        e_idx = jnp.argmax(probs, axis=-1)
        mask = jax.nn.one_hot(e_idx, E, dtype=x.dtype)
        token_priority = jnp.cumsum(mask[:, None, :], axis=-2)[:, 0, :]
        mask = mask * (token_priority <= EXPERT_CAPACITY).astype(x.dtype)
        combine = mask * p[:, None]

        def body(acc, ew):
            Wi_e, Wo_e, w_e = ew
            h = jax.nn.relu(x @ Wi_e) @ Wo_e
            return (acc + w_e[:, None] * h, None)
        out, _ = jax.lax.scan(body, jnp.zeros_like(x), (wi, wo, combine.T))
        return out.reshape(B, S, d)
    h = _L0_tok_ref(x, L0_tok_W, L0_tok_b)
    h = jnp.concatenate([jnp.broadcast_to(cls_tok, (h.shape[0], 1, h.shape[2])), h], axis=1)
    h = h + _L0_attn_ref(_layernorm(h, axis=-1), L0_attn_w_qkv, L0_attn_b_qkv, L0_attn_w_l, L0_attn_b_l, L0_attn_w_w, L0_attn_b_w, L0_attn_w_proj, L0_attn_b_proj)
    h = h + _L0_ffn_ref(_layernorm(h, axis=-1), L0_ffn_norm_scale, L0_ffn_gate_w, L0_ffn_gate_b, L0_ffn_mlp1_w, L0_ffn_mlp1_b, L0_ffn_mlp2_w, L0_ffn_mlp2_b)
    h = h + _L1_attn_ref(_layernorm(h, axis=-1), L1_attn_Wb, L1_attn_bb, L1_attn_Wd, L1_attn_bd, L1_attn_Wi, L1_attn_bi, L1_attn_gamma, L1_attn_beta)
    h = h + _L1_ffn_ref(_layernorm(h, axis=-1), L1_ffn_router_w, L1_ffn_wi, L1_ffn_wo)
    return h

_drawn_inputs = setup_inputs


def setup_inputs(seed=0):
    import zlib

    import numpy as np

    out = dict(_drawn_inputs(seed))
    spreads = {'L0_attn_b_qkv': (0.0, 0.1),
     'L0_attn_b_l': (0.0, 0.8),
     'L0_attn_b_w': (0.0, 0.1),
     'L0_attn_b_proj': (0.0, 0.1),
     'L0_ffn_norm_scale': (1.0, 0.6),
     'L0_ffn_gate_b': (0.0, 0.711),
     'L1_attn_bb': (0.0, 0.1),
     'L1_attn_gamma': (1.0, 0.2),
     'L1_attn_beta': (0.0, 0.1)}
    factors = {'L0_ffn_gate_w': 3.778,
     'L0_ffn_mlp1_w': 3.262,
     'L0_ffn_mlp1_b': 8.0,
     'L0_ffn_mlp2_w': 3.211,
     'L0_ffn_mlp2_b': 8.0}
    for name, (base, spread) in spreads.items():
        noise = np.random.default_rng([zlib.crc32(name.encode()), seed]).standard_normal(out[name].shape)
        drawn = base * np.exp(spread * noise) if base else spread * noise
        out[name] = jnp.asarray(drawn.astype(out[name].dtype))
    for name, factor in factors.items():
        out[name] = (out[name] * factor).astype(out[name].dtype)
    return out
```

```python
from contextlib import ExitStack

import concourse.bass as bass
from concourse import mybir

F32 = mybir.dt.float32
F32R = mybir.dt.float32r
BF16 = mybir.dt.bfloat16
ALU = mybir.AluOpType
ACT = mybir.ActivationFunctionType
AX_X = mybir.AxisListType.X

IMAGES, PATCHES, DIM = 32, 16, 192
SEQ = PATCHES + 1
TOKENS = IMAGES * SEQ
IMG_TILE = 7
TILE = IMG_TILE * SEQ
NTILES = -(-IMAGES // IMG_TILE)
TILE_IMGS = [min(IMG_TILE, IMAGES - IMG_TILE * i) for i in range(NTILES)]
ROWS = [n * SEQ for n in TILE_IMGS]
HALF = TOKENS // 2
KA, KB = 128, DIM - 128
PIX = 768
PIXC = PIX // 128
HEADS, HDIM = 12, 16
HG = HEADS // 2
HROWS = HG * SEQ
E0, F0, TOPK = 16, 384, 4
E1, F1 = 8, 768
C0, C1 = F0 // 128, F1 // 128
W1C = 768
W2C0, W2C1 = C0 * DIM, C1 * DIM
NBLK = DIM // 3
LIMIT = 7.0
EPS = 1e-5
PI = 3.14159265358979
TWO_PI_HI = 6.28125
TWO_PI_LO = 2 * PI - TWO_PI_HI
MAGIC = 12582912.0


def layout(blocks):
    at, out = 0, {}
    for name, n in blocks:
        out[name] = (at, n)
        at += n
    return out, at


PK1, PK1_COLS = layout([
    ("ident", 128), ("wqkv_a", 3 * DIM), ("wqkv_b", 3 * DIM), ("bqk", 4), ("wl", 2 * HEADS), ("bl", 2),
    ("ww", 2 * HEADS), ("delta", SEQ), ("mask", IMG_TILE), ("wp_a", DIM), ("wp_b", DIM)])
PK2, PK2_COLS = layout([
    ("scale", DIM), ("gate_a", E0), ("gate_b", E0), ("b1", E0 * 6), ("tri0", E0 * E0),
    ("wall_a", 7 * NBLK), ("wall_b", 7 * NBLK), ("ball", 7), ("gamma", DIM), ("beta", DIM),
    ("sel", NBLK), ("rout_a", E1), ("rout_b", E1), ("tri1", E1 * E1)])
RW, RW_COLS = layout([
    ("ind", TOKENS), ("tokb", DIM), ("ones", 128), ("bv", DIM), ("bp", DIM), ("bw", HEADS * SEQ),
    ("gb", E0), ("b2", DIM)])


def build(nc, xp, tokw, rows, pk1, pk2, w0, w1, out):
    ctx = ExitStack()
    with ctx:
        def sb(name, shape, dt=F32, stack=ctx):
            return stack.enter_context(nc.sbuf_tensor(name, shape, dt))

        def sem(name):
            return ctx.enter_context(nc.semaphore(name))

        pk2_sb = sb("pk2_sb", [128, PK2_COLS])
        rows_sb = sb("rows_sb", [16, RW_COLS])
        ident = sb("ident", [128, 128])
        h = sb("h", [128, NTILES, DIM])
        xn = sb("xn", [128, NTILES, DIM])
        xw = sb("xw", [128, NTILES, DIM])
        xt = sb("xt", [128, 2, TOKENS])
        stats = sb("stats", [128, NTILES, 6])
        mv = sb("mv", [128, NTILES, 2])
        sd = sb("sd", [128, NTILES])
        rstd = sb("rstd", [128, NTILES])
        ssq = sb("ssq", [128, NTILES])
        gl = sb("gl", [128, NTILES, E0])
        gmax = sb("gmax", [128, NTILES])
        gsum = sb("gsum", [128, NTILES])
        grec = sb("grec", [128, NTILES])
        gexp = sb("gexp", [128, NTILES, E0])
        rank = sb("rank", [128, NTILES, E0])
        comb = sb("comb", [128, NTILES, E0])
        eps_t = sb("eps_t", [128, 1])
        hpi_t = sb("hpi_t", [128, 1])
        eps_col, half_pi_col = eps_t[:, 0:1], hpi_t[:, 0:1]
        comb_t = sb("comb_t", [16, NTILES, 128])
        b1x = sb("b1x", [128, E0 * 6])

        xa_hi = sb("xa_hi", [128, TOKENS], F32R)
        xa_lo = sb("xa_lo", [128, TOKENS], F32R)
        xb_hi = sb("xb_hi", [128, TOKENS], F32R)
        xb_hl = sb("xb_hl", [128, TOKENS], F32R)
        raw1 = [sb(f"raw1_{k}", [128, 2 * W1C]) for k in range(2)]
        raw2 = [sb(f"raw2_{k}", [128, W2C1]) for k in range(2)]
        w1_hi = [sb(f"w1_hi{k}", [128, 2 * W1C], F32R) for k in range(2)]
        w1_lo = [sb(f"w1_lo{k}", [128, 2 * W1C], F32R) for k in range(2)]

        early = ExitStack()
        pk1_sb = sb("pk1_sb", [128, PK1_COLS], stack=early)
        xp_sb = sb("xp_sb", [128, PIXC * TOKENS], stack=early)
        tokw_sb = sb("tokw_sb", [128, PIXC, DIM], stack=early)
        q_sb = sb("q_sb", [128, 2, TOKENS], stack=early)
        k_sb = sb("k_sb", [128, 2, TOKENS], stack=early)
        v_sb = sb("v_sb", [128, NTILES, DIM], stack=early)
        lg = sb("lg", [128, 4, HALF], stack=early)
        prob = sb("prob", [128, 4, HALF], stack=early)
        smax = sb("smax", [128, 4, IMAGES // 2], stack=early)
        ssum = sb("ssum", [128, 4, IMAGES // 2], stack=early)
        srec = sb("srec", [128, 4, IMAGES // 2], stack=early)
        wmix = sb("wmix", [128, 2, HG * 2, SEQ], stack=early)
        abd = [sb(f"abd{k}", [128, HEADS, TILE], stack=early) for k in range(2)]
        qg = sb("qg", [128, 2, IMAGES, HEADS * SEQ], stack=early)
        early.close()
        scan = ExitStack()
        bvec = sb("bvec", [128, 3, HALF], stack=scan)
        bsq = sb("bsq", [128, 3, HALF], stack=scan)
        qv = sb("qv", [128, 3, HALF], stack=scan)
        dq = sb("dq", [128, 3, HALF], stack=scan)
        wq = sb("wq", [128, 3, HALF], stack=scan)
        qq = sb("qq", [128, 3, HALF], stack=scan)
        qx = sb("qx", [128, 3, HALF], stack=scan)
        dec = sb("dec", [128, HALF], stack=scan)
        norm = sb("norm", [128, HALF], stack=scan)
        rnorm = sb("rnorm", [128, HALF], stack=scan)
        half_ang = sb("half_ang", [128, HALF], stack=scan)
        turns = sb("turns", [128, HALF], stack=scan)
        habs = sb("habs", [128, HALF], stack=scan)
        sin_h = sb("sin_h", [128, HALF], stack=scan)
        cos_h = sb("cos_h", [128, HALF], stack=scan)
        rmat = sb("rmat", [128, SEQ, 3, 4, IMAGES // 2], stack=scan)
        hs = sb("hs", [128, SEQ, 4, IMAGES // 2], stack=scan)
        prod = sb("prod", [128, 3, 4, IMAGES // 2], stack=scan)
        hz = sb("hz", [128, 3, TOKENS], stack=scan)
        scan.close()
        hid_hi = [sb(f"hid_hi{k}", [128, C1, TOKENS], F32R) for k in range(2)]
        hid_lo = [sb(f"hid_lo{k}", [128, C1, TOKENS], F32R) for k in range(2)]
        w2_hi = [sb(f"w2_hi{k}", [128, W2C1], F32R) for k in range(2)]
        w2_lo = [sb(f"w2_lo{k}", [128, W2C1], F32R) for k in range(2)]
        lin = sb("lin", [128, C0, TOKENS])
        cmp_a = sb("cmp_a", [128, NTILES, E0, E0], BF16)
        cmp_b = sb("cmp_b", [128, NTILES, E0, E0], BF16)
        glu = sb("glu", [128, C0, TOKENS])
        gact = sb("gact", [128, C0, TOKENS])
        aval = sb("aval", [128, C0, TOKENS])

        ps = ctx.enter_context(nc.psum_tensor("ps", [128, 8, 512], F32))

        def p1(name, r=128):
            a, n = PK1[name]
            return pk1_sb[0:r, a:a + n]

        def p2(name, r=128):
            a, n = PK2[name]
            return pk2_sb[0:r, a:a + n]

        def rw(name, r=1):
            a, n = RW[name]
            return rows_sb[0:r, a:a + n]

        def tile_cols(i):
            return slice(TILE * i, TILE * i + ROWS[i])

        tokw_in, rows_in, pk1_in, pk2_in, ident_in = (sem(n) for n in ("tokw_in", "rows_in", "pk1_in", "pk2_in", "ident_in"))
        xp_in = [sem(f"xp_in{i}") for i in range(NTILES)]
        cleared = sem("cleared")
        tok_mm, h0_ready = sem("tok_mm"), sem("h0_ready")
        ln = [dict(stat=sem(f"ln{k}_stat"), mean=sem(f"ln{k}_mean"), sd=sem(f"ln{k}_sd"), rs=sem(f"ln{k}_rs"),
                   xn=sem(f"ln{k}_xn")) for k in range(5)]
        tr = [dict(mm=sem(f"tr{k}_mm"), act=sem(f"tr{k}_act"), dve=sem(f"tr{k}_dve")) for k in range(5)]
        qk_mm, q_ready, k_ready, v_mm, v_ready = (sem(n) for n in ("qk_mm", "q_ready", "k_ready", "v_mm", "v_ready"))
        qg_dve, qg_act, sc_mm, lg_ready = (sem(n) for n in ("qg_dve", "qg_act", "sc_mm", "lg_ready"))
        smax_ready, lg_shift, exp_ready, ssum_ready, srec_ready, prob_ready = (
            sem(n) for n in ("smax_ready", "lg_shift", "exp_ready", "ssum_ready", "srec_ready", "prob_ready"))
        wmix_ready, mix_mm, abd_ready, av_mm, o_ready, proj_mm, h1_ready = (
            sem(n) for n in ("wmix_ready", "mix_mm", "abd_ready", "av_mm", "o_ready", "proj_mm", "h1_ready"))
        ssq_ready, rms_sd, rms_rs, t_ready = (sem(n) for n in ("ssq_ready", "rms_sd", "rms_rs", "t_ready"))
        xhi = [sem(f"xhi{k}") for k in range(2)]
        xlo = [sem(f"xlo{k}") for k in range(2)]
        xhl = [sem(f"xhl{k}") for k in range(2)]
        rt = [dict(mm=sem(f"rt{k}_mm"), step=sem(f"rt{k}_step"), shift=sem(f"rt{k}_shift"), exp=sem(f"rt{k}_exp"),
                   comb=sem(f"rt{k}_comb")) for k in range(2)]
        b1_ready, hx_ready = sem("b1_ready"), sem("hx_ready")
        ct_mm, ct_ready, b2_mm, base_ready = (sem(n) for n in ("ct_mm", "ct_ready", "b2_mm", "base_ready"))
        moe = [dict(raw1=[sem(f"m{k}_raw1_{j}") for j in range(2)], raw2=[sem(f"m{k}_raw2_{j}") for j in range(2)],
                    **{n: sem(f"m{k}_{n}") for n in ("w1_hi", "w1_lo", "w2_hi", "w2_lo", "up", "glu", "lin", "clamp",
                                                     "gact", "aval", "hid_hi", "hid_lo", "down", "y")})
               for k in range(2)]
        wall_mm, bvec_ready, dec_ready, inj_ready = (sem(n) for n in ("wall_mm", "bvec_ready", "dec_ready", "inj_ready"))
        nsq_ready, norm_ready, ang_ready, sin_ready, rot_step, scan_step, scan_done = (
            sem(n) for n in ("nsq_ready", "norm_ready", "ang_ready", "sin_ready", "rot_step", "scan_step", "scan_done"))
        base2_ready, hz_act, hz_dve, ht_mm, ht_ready, h3_ready = (
            sem(n) for n in ("base2_ready", "hz_act", "hz_dve", "ht_mm", "ht_ready", "h3_ready"))
        stored = sem("stored")

        LAYERS = [
            dict(E=E0, C=C0, W2=W2C0, dram=w0, s=moe[0]),
            dict(E=E1, C=C1, W2=W2C1, dram=w1, s=moe[1]),
        ]

        def periods(eng, n_experts, period):
            period(0, 0, 0, 0, True, True)
            period(1, 1, 0, 1, True, True)
            with eng.Fori(0, n_experts // 2 - 2) as i:
                period(2 * i + 2, 0, i + 1, 2, True, True)
                period(2 * i + 3, 1, i + 1, 2, True, True)
            period(n_experts - 2, 0, n_experts // 2 - 1, 2, True, True)
            period(n_experts - 1, 1, n_experts // 2 - 1, 2, True, False)
            period(n_experts, 0, n_experts // 2, 2, False, False)

        block = ctx.enter_context(nc.Block())

        @block.sync
        def _(sp):
            sp.dma_start(tokw_sb[:], tokw.rearrange("p (c d) -> p c d", d=DIM)).then_inc(tokw_in, 16)
            for i in range(NTILES):
                cols = slice(PIXC * TILE * i, PIXC * (TILE * i + ROWS[i]))
                sp.dma_start(xp_sb[:, cols], xp[:, cols]).then_inc(xp_in[i], 16)
                if i == 0:
                    sp.dma_start(rows_sb[:], rows).then_inc(rows_in, 16)

            def load1(layer, dram, e, k):
                sp.dma_start(raw1[k][:], dram[bass.ds(e, 1), :, 0:2 * W1C].rearrange("a p c -> (a p) c"))\
                  .then_inc(layer["s"]["raw1"][k], 16)

            def load2(layer, dram, e, k):
                n = layer["W2"]
                sp.dma_start(raw2[k][:, 0:n], dram[bass.ds(e, 1), :, 2 * W1C:2 * W1C + n].rearrange("a p c -> (a p) c"))\
                  .then_inc(layer["s"]["raw2"][k], 16)

            for n, layer in enumerate(LAYERS):
                s = layer["s"]
                for k in range(2):
                    if n:
                        sp.wait_ge(LAYERS[0]["s"]["w1_hi"], 2 * (E0 - 1 + k))
                        sp.wait_ge(LAYERS[0]["s"]["w1_lo"], 2 * (E0 - 1 + k))
                    load1(layer, layer["dram"], k, k)
                    if n:
                        sp.wait_ge(LAYERS[0]["s"]["w2_hi"], E0 - 1 + k)
                        sp.wait_ge(LAYERS[0]["s"]["w2_lo"], E0 - 1 + k)
                    load2(layer, layer["dram"], k, k)
                with sp.Fori(0, layer["E"] // 2 - 1) as i:
                    for k in range(2):
                        sp.wait_ge(s["w1_hi"], 4 * i + 2 * k + 2)
                        sp.wait_ge(s["w1_lo"], 4 * i + 2 * k + 2)
                        load1(layer, layer["dram"], 2 * i + 2 + k, k)
                        sp.wait_ge(s["w2_hi"], 2 * i + k + 1)
                        sp.wait_ge(s["w2_lo"], 2 * i + k + 1)
                        load2(layer, layer["dram"], 2 * i + 2 + k, k)
            for i in range(NTILES):
                sp.wait_ge(moe[1]["y"], NTILES * (E1 - 1) + i + 1)
                sp.dma_start(out[tile_cols(i), :], h[0:ROWS[i], i, :]).then_inc(stored, 16)
            sp.wait_ge(stored, 16 * NTILES)

        @block.scalar
        def _(act):
            act.dma_start(ident[:], pk1[:, 0:128]).then_inc(ident_in, 16)
            act.dma_start(pk1_sb[:], pk1).then_inc(pk1_in, 16)
            act.dma_start(pk2_sb[:], pk2).then_inc(pk2_in, 16)

            def root(k):
                act.wait_ge(ln[k]["mean"], NTILES)
                act.wait_ge(cleared, 6)
                act.activation(sd[:], mv[:, :, 1], ACT.Sqrt, bias=eps_col).then_inc(ln[k]["sd"], 1)

            def evac_transposed(k, b0, n=KB):
                act.wait_ge(tr[k]["mm"], NTILES)
                act.activation(xt[:, 0, 0:4 * TILE].rearrange("p (t c) -> p t c", t=4),
                               ps[:, b0, :].rearrange("p (t c) -> p t c", t=4)[:, :, 0:TILE], ACT.Copy)\
                   .then_inc(tr[k]["act"], 1)
                act.activation(xt[:, 0, 4 * TILE:TOKENS], ps[:, b0 + 2, 0:ROWS[4]], ACT.Copy).then_inc(tr[k]["act"], 1)
                act.activation(xt[0:n, 1, 4 * TILE:TOKENS], ps[0:n, b0 + 2, 128:128 + ROWS[4]], ACT.Copy)\
                   .then_inc(tr[k]["act"], 1)

            def split_x(k, t):
                act.wait_ge(tr[t]["act"], 3)
                act.wait_ge(tr[t]["dve"], 1)
                act.activation(xa_hi[:], xt[:, 0, :], ACT.Copy).then_inc(xhi[k], 1)
                act.activation(xb_hi[:], xt[:, 1, :], ACT.Copy).then_inc(xhi[k], 1)
                act.activation(xb_hl[0:64, :], xt[0:64, 1, :], ACT.Copy).then_inc(xhi[k], 1)

            def split_w1(layer, e, k, pair, reused):
                s = layer["s"]
                act.wait_ge(s["raw1"][k], 16 * pair + 16)
                if reused:
                    act.wait_ge(s["up"], 6 * e - 6)
                for a in (0, W1C):
                    act.activation(w1_hi[k][:, a:a + W1C], raw1[k][:, a:a + W1C], ACT.Copy).then_inc(s["w1_hi"], 1)

            def split_w2(layer, e, k, pair, reused):
                s = layer["s"]
                act.wait_ge(s["raw2"][k], 16 * pair + 16)
                if reused:
                    act.wait_ge(s["down"], NTILES * e - NTILES)
                act.activation(w2_hi[k][:, 0:layer["W2"]], raw2[k][:, 0:layer["W2"]], ACT.Copy).then_inc(s["w2_hi"], 1)

            for i, r in enumerate(ROWS):
                act.wait_ge(tok_mm, i + 1)
                if i == 0:
                    act.wait_ge(cleared, 6)
                act.activation(h[0:r, i, :], ps[0:r, i, 0:DIM], ACT.Copy).then_inc(h0_ready, 1)
            root(0)
            evac_transposed(0, 5)

            act.wait_ge(pk1_in, 16)
            for c, K in ((0, KA), (1, KB)):
                act.wait_ge(qk_mm, 2 * c + 2)
                act.activation(k_sb[0:K, c, :].rearrange("p (a b) -> p a b", a=2), ps[0:K, 4 * c + 2:4 * c + 4, 0:HALF],
                               ACT.Identity, bias=p1("bqk")[0:K, 2 + c:3 + c]).then_inc(k_ready, 1)
            act.wait_ge(q_ready, 2)
            for g in range(HG):
                act.activation(qg[0:KB, 1, :, g * SEQ:(g + 1) * SEQ], q_sb[0:KB, 1, :].rearrange("p (b n) -> p b n", n=SEQ),
                               ACT.Copy, scale=p1("wl")[0:KB, HEADS + g:HEADS + g + 1]).then_inc(qg_act, 1)
            for i, r in enumerate(ROWS):
                act.wait_ge(v_mm, i + 1)
                act.activation(v_sb[0:r, i, :], ps[0:r, i, 0:DIM], ACT.Copy).then_inc(v_ready, 1)

            for n in range(5):
                if n < 4:
                    act.wait_ge(sc_mm, n + 1)
                    act.activation(lg[0:HROWS, n, :], ps[0:HROWS, n, 0:HALF], ACT.Identity,
                                   bias=p1("bl")[0:HROWS, n // 2:n // 2 + 1]).then_inc(lg_ready, 1)
                if n:
                    act.wait_ge(lg_shift, n)
                    act.activation(prob[0:HROWS, n - 1, :], lg[0:HROWS, n - 1, :], ACT.Exp).then_inc(exp_ready, 1)

            split_w1(LAYERS[0], 0, 0, 0, False)

            for i, r in enumerate(ROWS):
                act.wait_ge(av_mm, i + 1)
                act.activation(xw[0:r, i, :], ps[0:r, 6 + i % 2, 0:DIM], ACT.Copy).then_inc(o_ready, 1)
            evac_transposed(1, 0)

            root(1)
            for i, r in enumerate(ROWS):
                act.wait_ge(ln[1]["xn"], i + 1)
                act.activation(xw[0:r, i, :], xn[0:r, i, :], ACT.Square, accum_out=ssq[0:r, i:i + 1]).then_inc(ssq_ready, 1)
            act.wait_ge(ssq_ready, NTILES)
            act.activation(sd[:], ssq[:], ACT.Sqrt, bias=eps_col, scale=1.0 / DIM).then_inc(rms_sd, 1)
            evac_transposed(2, 0, 128)
            split_x(0, 2)

            def exps(k, E):
                act.wait_ge(rt[k]["shift"], 1)
                act.activation(gexp[:, :, 0:E], gexp[:, :, 0:E], ACT.Exp).then_inc(rt[k]["exp"], 1)


            def period0(p, k, pair, age, has_up, has_next):
                layer, s = LAYERS[0], moe[0]

                def linear(j):
                    act.wait_ge(s["up"], 6 * p + 2 * j + 2)
                    if age:
                        act.wait_ge(s["aval"], C0 * p - C0 + j + 1)
                    slot = 2 * ((2 * j + 1) % 3)
                    act.activation(lin[:, j, :].rearrange("p (a b) -> p a b", a=2), ps[:, slot:slot + 2, 0:HALF],
                                   ACT.Identity, bias=b1x[:, bass.ds(6 * p + 3 + j, 1)]).then_inc(s["lin"], 1)

                def gated(j):
                    act.wait_ge(s["glu"], C0 * p + j + 1)
                    if age:
                        act.wait_ge(s["aval"], C0 * p - C0 + j + 1)
                    act.activation(gact[:, j, :], glu[:, j, :], ACT.Gelu_apprx_sigmoid).then_inc(s["gact"], 1)

                def high(j):
                    act.wait_ge(s["aval"], C0 * p + j + 1)
                    if age > 1:
                        act.wait_ge(s["down"], NTILES * p - NTILES)
                    act.activation(hid_hi[k][:, j, :], aval[:, j, :], ACT.Copy).then_inc(s["hid_hi"], 1)

                if has_up:
                    linear(0)
                    gated(0)
                    linear(1)
                    gated(1)
                    high(0)
                    linear(2)
                    gated(2)
                    split_w2(layer, p, k, pair, age > 1)
                    high(1)
                    high(2)
                if has_next:
                    split_w1(layer, p + 1, 1 - k, pair + k, age > 0)
                if age == 0:
                    exps(0, E0)
                    act.wait_ge(ct_mm, NTILES)
                    act.activation(comb_t[:, 0:4, 0:TILE], ps[0:E0, 7, :].rearrange("p (t c) -> p t c", t=4)[:, :, 0:TILE],
                                   ACT.Copy).then_inc(ct_ready, 1)
                    act.activation(comb_t[:, 4, 0:ROWS[4]], ps[0:E0, 6, 0:ROWS[4]], ACT.Copy).then_inc(ct_ready, 1)

            periods(act, E0, period0)

            root(2)
            evac_transposed(3, 5)
            split_w1(LAYERS[1], 0, 0, 0, False)
            halves = "p (b t) -> p b t"
            for c in range(3):
                act.wait_ge(wall_mm, c + 1)
                act.activation(bvec[:, c, :], ps[:, c, 0:HALF], ACT.Identity, bias=p2("ball")[:, c:c + 1])\
                   .then_inc(bvec_ready, 1)
            act.wait_ge(wall_mm, 4)
            act.activation(dec[:], ps[:, 6, 0:HALF], ACT.Sigmoid, bias=p2("ball")[:, 6:7]).then_inc(dec_ready, 1)
            act.wait_ge(nsq_ready, 1)
            act.activation(norm[:], norm[:], ACT.Sqrt).then_inc(norm_ready, 1)
            for c in range(3):
                act.wait_ge(wall_mm, 5 + c)
                act.activation(rmat[:, :, c, 3, :].rearrange("p t b -> p b t"),
                               ps[:, 3 + c, 0:HALF].rearrange(halves, t=SEQ), ACT.Identity,
                               bias=p2("ball")[:, 3 + c:4 + c]).then_inc(inj_ready, 1)
            act.wait_ge(ang_ready, 2)
            act.activation(sin_h[:], half_ang[:], ACT.Sin).then_inc(sin_ready, 1)
            act.activation(cos_h[:], habs[:], ACT.Sin, scale=-1.0, bias=half_pi_col).then_inc(sin_ready, 1)
            act.wait_ge(scan_done, 1)
            act.wait_ge(hx_ready, NTILES + 1)
            for c in range(3):
                act.activation(hz[0:64, c, 0:HALF].rearrange(halves, t=SEQ),
                               hs[0:64, :, c, :].rearrange("p t b -> p b t"), ACT.Copy).then_inc(hz_act, 1)
            for i, r in enumerate(ROWS):
                act.wait_ge(ht_mm, i + 1)
                act.activation(xw[0:r, i, :].rearrange("p (b c) -> p c b", c=3),
                               ps[0:r, i, 0:DIM].rearrange("p (c b) -> p c b", c=3), ACT.Copy).then_inc(ht_ready, 1)
            root(3)
            root(4)
            evac_transposed(4, 5, 128)
            split_x(1, 4)
            exps(1, E1)

            def period1(p, k, pair, age, has_up, has_next):
                layer, s = LAYERS[1], moe[1]
                for j in range(C1 if has_up else 0):
                    act.wait_ge(s["up"], 6 * p + j + 1)
                    if j == 0 and age > 1:
                        act.wait_ge(s["down"], NTILES * p - NTILES)
                    slot = 2 * (j % 3)
                    act.activation(hid_hi[k][:, j, :].rearrange("p (a b) -> p a b", a=2), ps[:, slot:slot + 2, 0:HALF],
                                   ACT.Relu).then_inc(s["hid_hi"], 1)
                    if j == 3:
                        split_w2(layer, p, k, pair, age > 1)
                if has_next:
                    split_w1(layer, p + 1, 1 - k, pair + k, age > 0)

            periods(act, E1, period1)

        @block.gpsimd
        def _(pool):
            pool.memset(eps_t[:], EPS).then_inc(cleared, 1)
            pool.memset(hpi_t[:], PI / 2).then_inc(cleared, 1)
            pool.memset(h[:], 0.0).then_inc(cleared, 1)
            pool.memset(mv[:], 1.0).then_inc(cleared, 1)
            pool.memset(ssq[:], 1.0).then_inc(cleared, 1)
            pool.memset(gl[:], 0.0).then_inc(cleared, 1)

            def low_w1(layer, e, k, pair, reused):
                s = layer["s"]
                if reused:
                    pool.wait_ge(s["up"], 6 * e - 6)
                for n, a in enumerate((0, W1C)):
                    pool.wait_ge(s["w1_hi"], 2 * e + n + 1)
                    pool.tensor_tensor(w1_lo[k][:, a:a + W1C], raw1[k][:, a:a + W1C], w1_hi[k][:, a:a + W1C].bitcast(F32),
                                       ALU.subtract).then_inc(s["w1_lo"], 1)

            def low_w2(layer, e, k, pair, reused):
                s, n = layer["s"], layer["W2"]
                if reused:
                    pool.wait_ge(s["down"], NTILES * e - NTILES)
                pool.wait_ge(s["w2_hi"], e + 1)
                pool.tensor_tensor(w2_lo[k][:, 0:n], raw2[k][:, 0:n], w2_hi[k][:, 0:n].bitcast(F32), ALU.subtract)\
                    .then_inc(s["w2_lo"], 1)

            def make_period(layer):
                def period(p, k, pair, age, has_up, has_next):
                    if has_up:
                        low_w2(layer, p, k, pair, age > 1)
                    if has_next:
                        low_w1(layer, p + 1, 1 - k, pair + k, age > 0)
                return period

            low_w1(LAYERS[0], 0, 0, 0, False)
            pool.wait_ge(ln[1]["xn"], NTILES)
            for i, r in enumerate(ROWS):
                pool.tensor_tensor(h[0:r, i, :], h[0:r, i, :], xn[0:r, i, :], ALU.add).then_inc(hx_ready, 1)
            periods(pool, E0, make_period(LAYERS[0]))
            low_w1(LAYERS[1], 0, 0, 0, False)
            pool.wait_ge(tr[3]["mm"], NTILES)
            pool.memset(hz[:], 0.0).then_inc(hx_ready, 1)
            pool.wait_ge(ln[2]["xn"], NTILES)
            for i, r in enumerate(ROWS):
                pool.tensor_tensor(h[0:r, i, :], h[0:r, i, :], xn[0:r, i, :], ALU.add).then_inc(hx_ready, 1)
                pool.wait_ge(hx_ready, NTILES + 2 + i)
                pool.tensor_tensor(h[0:r, i, :], h[0:r, i, :], p2("beta", r), ALU.add).then_inc(base2_ready, 1)
            periods(pool, E1, make_period(LAYERS[1]))

        @block.vector
        def _(dve):
            def layer_norm(k, src, ready):
                s = ln[k]
                for i, r in enumerate(ROWS):
                    ready(i)
                    dve.bn_stats(stats[0:r, i, :], src[0:r, i, :]).then_inc(s["stat"], 1)
                for i, r in enumerate(ROWS):
                    dve.wait_ge(s["stat"], i + 1)
                    dve.bn_aggr(mv[0:r, i, :], stats[0:r, i, :]).then_inc(s["mean"], 1)
                dve.wait_ge(s["sd"], 1)
                dve.reciprocal(rstd[:], sd[:]).then_inc(s["rs"], 1)
                dve.wait_ge(s["rs"], 1)
                dst = xw if k == 3 else xn
                for i, r in enumerate(ROWS):
                    dve.tensor_scalar(dst[0:r, i, :], src[0:r, i, :], mv[0:r, i, 0:1], rstd[0:r, i:i + 1], ALU.subtract,
                                      ALU.mult).then_inc(s["xn"], 1)

            def evac_transposed(k, b0, n=KB):
                dve.wait_ge(tr[k]["mm"], NTILES)
                dve.tensor_copy(xt[0:n, 1, 0:4 * TILE].rearrange("p (t c) -> p t c", t=4),
                                ps[0:n, b0 + 1, :].rearrange("p (t c) -> p t c", t=4)[:, :, 0:TILE]).then_inc(tr[k]["dve"], 1)

            def split_x(k):
                dve.wait_ge(xhi[k], 1)
                dve.tensor_tensor(xa_lo[:], xt[:, 0, :], xa_hi[:].bitcast(F32), ALU.subtract).then_inc(xlo[k], 1)
                dve.wait_ge(xhi[k], 2)
                dve.tensor_tensor(xb_hl[64:128, :], xt[64:128, 1, :], xb_hi[64:128, :].bitcast(F32), ALU.subtract)\
                   .then_inc(xlo[k], 1)

            def route(k, E, top, on_probs):
                s, n = rt[k], [0]

                def step(ins):
                    n[0] += 1
                    ins.then_inc(s["step"], 1)
                    dve.wait_ge(s["step"], n[0])

                g, x = gl[:, :, 0:E], gexp[:, :, 0:E]
                a, b = cmp_a[:, :, 0:E, 0:E], cmp_b[:, :, 0:E, 0:E]
                over = [128, NTILES, E]
                dve.wait_ge(s["mm"], NTILES)
                bank = ps[:, 6, 0:NTILES * E].rearrange("p (t e) -> p t e", e=E)
                step(dve.tensor_copy(gl[0:TILE, 0:4, 0:E], bank[0:TILE, 0:4, :]))
                step(dve.tensor_copy(gl[0:ROWS[4], 4, 0:E], bank[0:ROWS[4], 4, :]))
                step(dve.tensor_reduce(gmax[:], g, AX_X, ALU.max))
                dve.tensor_tensor(x, g, gmax[:].unsqueeze(2).to_broadcast(over), ALU.subtract).then_inc(s["shift"], 1)
                dve.wait_ge(s["exp"], 1)

                def normalize(v):
                    step(dve.tensor_reduce(gsum[:], v, AX_X, ALU.add))
                    step(dve.reciprocal(grec[:], gsum[:]))

                key = g
                if on_probs:
                    normalize(x)
                    step(dve.tensor_tensor(x, x, grec[:].unsqueeze(2).to_broadcast(over), ALU.mult))
                    key = x
                every = [128, NTILES, E, E]
                other, own = key.unsqueeze(2).to_broadcast(every), key.unsqueeze(3).to_broadcast(every)
                below = p2(f"tri{k}").rearrange("p (i j) -> p i j", i=E).unsqueeze(1).to_broadcast(every)
                step(dve.tensor_tensor(b, other, own, ALU.is_ge))
                step(dve.tensor_tensor(b, b, below, ALU.mult))
                step(dve.tensor_tensor(a, other, own, ALU.is_gt))
                step(dve.tensor_tensor(a, a, b, ALU.max))
                step(dve.tensor_reduce(rank[:, :, 0:E], a, AX_X, ALU.add))
                c = comb[:, :, 0:E]
                last = dve.scalar_tensor_tensor(c, rank[:, :, 0:E], float(top), x, ALU.is_lt, ALU.mult)
                if not on_probs:
                    step(last)
                    normalize(c)
                    last = dve.tensor_tensor(c, c, grec[:].unsqueeze(2).to_broadcast(over), ALU.mult)
                last.then_inc(s["comb"], 1)

            layer_norm(0, h, lambda i: dve.wait_ge(h0_ready, i + 1))
            evac_transposed(0, 5)

            dve.wait_ge(pk1_in, 16)
            delta = p1("delta", HROWS).unsqueeze(1).to_broadcast([HROWS, 2 * HEADS, SEQ])
            dve.tensor_tensor(wmix[0:HROWS].rearrange("p a g n -> p (a g) n"),
                              p1("ww", HROWS).unsqueeze(2).to_broadcast([HROWS, 2 * HEADS, SEQ]), delta, ALU.mult)\
               .then_inc(wmix_ready, 1)
            for c, K in ((0, KA), (1, KB)):
                dve.wait_ge(qk_mm, 2 * c + 1)
                dve.tensor_scalar(q_sb[0:K, c, :].rearrange("p (a b) -> p a b", a=2), ps[0:K, 4 * c:4 * c + 2, 0:HALF],
                                  p1("bqk")[0:K, c:c + 1], HDIM ** -0.5, ALU.add, ALU.mult).then_inc(q_ready, 1)
            dve.wait_ge(q_ready, 2)
            for c, K, g0 in ((0, KA, 0), (0, KA, HG), (1, KB, HG)):
                for g in range(g0, g0 + HG):
                    dve.tensor_scalar(qg[0:K, c, :, g * SEQ:(g + 1) * SEQ], q_sb[0:K, c, :].rearrange("p (b n) -> p b n", n=SEQ),
                                      p1("wl")[0:K, HEADS * c + g:HEADS * c + g + 1], None, ALU.mult).then_inc(qg_dve, 1)

            for n in range(5):
                by = [HROWS, IMAGES // 2, SEQ]
                if n < 4:
                    x = lg[0:HROWS, n, :].rearrange("p (b m) -> p b m", m=SEQ)
                    dve.wait_ge(lg_ready, n + 1)
                    dve.tensor_reduce(smax[0:HROWS, n, :], x, AX_X, ALU.max).then_inc(smax_ready, 1)
                    dve.wait_ge(smax_ready, n + 1)
                    dve.tensor_tensor(x, x, smax[0:HROWS, n, :].unsqueeze(2).to_broadcast(by), ALU.subtract)\
                       .then_inc(lg_shift, 1)
                if n:
                    y = prob[0:HROWS, n - 1, :].rearrange("p (b m) -> p b m", m=SEQ)
                    dve.wait_ge(exp_ready, n)
                    dve.tensor_reduce(ssum[0:HROWS, n - 1, :], y, AX_X, ALU.add).then_inc(ssum_ready, 1)
                    dve.wait_ge(ssum_ready, n)
                    dve.reciprocal(srec[0:HROWS, n - 1, :], ssum[0:HROWS, n - 1, :]).then_inc(srec_ready, 1)
                    dve.wait_ge(srec_ready, n)
                    dve.tensor_tensor(y, y, srec[0:HROWS, n - 1, :].unsqueeze(2).to_broadcast(by), ALU.mult)\
                       .then_inc(prob_ready, 1)

            for i, r in enumerate(ROWS):
                dve.wait_ge(mix_mm, i + 1)
                if i >= 2:
                    dve.wait_ge(av_mm, i - 1)
                ni = TILE_IMGS[i]
                by = [r, HEADS, ni, SEQ]
                dve.tensor_tensor(abd[i % 2][0:r, :, 0:r].rearrange("p g (b n) -> p g b n", n=SEQ),
                                  ps[0:r, 4 + i % 2, 0:HEADS * SEQ].rearrange("p (g n) -> p g n", n=SEQ).unsqueeze(2)
                                  .to_broadcast(by),
                                  p1("mask", r)[:, 0:ni].unsqueeze(1).unsqueeze(3).to_broadcast(by), ALU.mult)\
                   .then_inc(abd_ready, 1)
            evac_transposed(1, 0)
            for i, r in enumerate(ROWS):
                dve.wait_ge(proj_mm, i + 1)
                dve.tensor_tensor(h[0:r, i, :], ps[0:r, 3 + i, 0:DIM], h[0:r, i, :], ALU.add).then_inc(h1_ready, 1)

            layer_norm(1, h, lambda i: dve.wait_ge(h1_ready, i + 1))
            dve.wait_ge(rms_sd, 1)
            dve.reciprocal(rstd[:], sd[:]).then_inc(rms_rs, 1)
            dve.wait_ge(rms_rs, 1)
            dve.wait_ge(pk2_in, 16)
            for i, r in enumerate(ROWS):
                dve.scalar_tensor_tensor(xw[0:r, i, :], xn[0:r, i, :], rstd[0:r, i:i + 1], p2("scale", r), ALU.mult, ALU.mult)\
                   .then_inc(t_ready, 1)
            b1v = b1x[:].rearrange("p (e j) -> p e j", j=6)
            p2b = p2("b1").rearrange("p (e j) -> p e j", j=6)
            dve.tensor_copy(b1v[:, :, 0:C0], p2b[:, :, 0:C0]).then_inc(b1_ready, 1)
            dve.tensor_scalar(b1v[:, :, C0:6], p2b[:, :, C0:6], 1.0, None, ALU.add).then_inc(b1_ready, 1)
            evac_transposed(2, 0, 128)
            split_x(0)

            def add_expert(s, p, k, i, age):
                r = ROWS[i]
                dve.wait_ge(s["down"], NTILES * p - NTILES + i + 1)
                if age > 1 or i:
                    dve.wait_ge(s["y"], NTILES * p - NTILES + i)
                bank = 6 + (NTILES * (1 - k) + i) % 2
                dve.scalar_tensor_tensor(h[0:r, i, :], ps[0:r, bank, 0:DIM], comb[0:r, i, bass.ds(p - 1, 1)],
                                         h[0:r, i, :], ALU.mult, ALU.add).then_inc(s["y"], 1)

            def period0(p, k, pair, age, has_up, has_next):
                s = moe[0]

                def gate(j):
                    dve.wait_ge(s["up"], 6 * p + 2 * j + 1)
                    if age:
                        dve.wait_ge(s["gact"], C0 * p - C0 + j + 1)
                    slot = 2 * ((2 * j) % 3)
                    dve.tensor_scalar(glu[:, j, :].rearrange("p (a b) -> p a b", a=2), ps[:, slot:slot + 2, 0:HALF],
                                      b1x[:, bass.ds(6 * p + j, 1)], LIMIT, ALU.add, ALU.min).then_inc(s["glu"], 1)

                def value(j):
                    dve.wait_ge(s["lin"], C0 * p + j + 1)
                    dve.tensor_scalar(lin[:, j, :], lin[:, j, :], 1.0 + LIMIT, 1.0 - LIMIT, ALU.min, ALU.max)\
                       .then_inc(s["clamp"], 1)
                    dve.wait_ge(s["clamp"], C0 * p + j + 1)
                    dve.wait_ge(s["gact"], C0 * p + j + 1)
                    if age:
                        dve.wait_ge(s["hid_lo"], C0 * p - C0 + j + 1)
                    dve.tensor_tensor(aval[:, j, :], gact[:, j, :], lin[:, j, :], ALU.mult).then_inc(s["aval"], 1)

                def low(j):
                    dve.wait_ge(s["hid_hi"], C0 * p + j + 1)
                    if age > 1:
                        dve.wait_ge(s["down"], NTILES * p - NTILES)
                    dve.tensor_tensor(hid_lo[k][:, j, :], aval[:, j, :], hid_hi[k][:, j, :].bitcast(F32), ALU.subtract)\
                       .then_inc(s["hid_lo"], 1)

                def add(i):
                    if age:
                        add_expert(s, p, k, i, age)

                if has_up:
                    gate(0)
                    gate(1)
                    value(0)
                    gate(2)
                    low(0)
                    value(1)
                add(0)
                if has_up:
                    low(1)
                    value(2)
                add(1)
                add(2)
                if has_up:
                    low(2)
                add(3)
                add(4)
                if age == 0:
                    route(0, E0, TOPK, False)
                    for i, r in enumerate(ROWS):
                        dve.wait_ge(b2_mm, i + 1)
                        dve.wait_ge(hx_ready, i + 1)
                        dve.tensor_tensor(h[0:r, i, :], ps[0:r, 6 + i % 2, 0:DIM], h[0:r, i, :], ALU.add)\
                           .then_inc(base_ready, 1)
                    dve.wait_ge(rt[0]["comb"], 1)
                    dve.wait_ge(base_ready, NTILES)

            dve.wait_ge(b1_ready, 2)
            periods(dve, E0, period0)

            layer_norm(2, h, lambda i: dve.wait_ge(moe[0]["y"], NTILES * (E0 - 1) + i + 1))
            evac_transposed(3, 5)
            n = [0]

            def step(ins):
                n[0] += 1
                ins.then_inc(rot_step, 1)
                dve.wait_ge(rot_step, n[0])

            step(dve.memset(hs[:, :, 3, :], 1.0))
            dve.wait_ge(bvec_ready, 3)
            step(dve.tensor_tensor(bsq[:], bvec[:], bvec[:], ALU.mult))
            step(dve.tensor_tensor(norm[:], bsq[:, 0, :], bsq[:, 1, :], ALU.add))
            dve.tensor_tensor(norm[:], norm[:], bsq[:, 2, :], ALU.add).then_inc(nsq_ready, 1)
            dve.wait_ge(norm_ready, 1)
            step(dve.tensor_scalar(norm[:], norm[:], 1e-8, None, ALU.max))
            step(dve.tensor_scalar(turns[:], norm[:], 0.25 / PI, MAGIC, ALU.mult, ALU.add))
            step(dve.tensor_scalar(turns[:], turns[:], MAGIC, None, ALU.subtract))
            step(dve.tensor_scalar(half_ang[:], norm[:], 0.5, None, ALU.mult))
            step(dve.scalar_tensor_tensor(half_ang[:], turns[:], -TWO_PI_HI, half_ang[:], ALU.mult, ALU.add))
            step(dve.scalar_tensor_tensor(half_ang[:], turns[:], -TWO_PI_LO, half_ang[:], ALU.mult, ALU.add))
            dve.tensor_scalar(half_ang[:], half_ang[:], 3.1415925, -3.1415925, ALU.min, ALU.max).then_inc(ang_ready, 1)
            dve.wait_ge(ang_ready, 1)
            dve.scalar_tensor_tensor(habs[:], half_ang[:], -1.0, half_ang[:], ALU.mult, ALU.max).then_inc(ang_ready, 1)
            step(dve.reciprocal(rnorm[:], norm[:]))
            dve.wait_ge(sin_ready, 1)
            step(dve.tensor_tensor(rnorm[:], rnorm[:], sin_h[:], ALU.mult))
            step(dve.tensor_tensor(qv[:, 0, :], bvec[:, 2, :], rnorm[:], ALU.mult))
            step(dve.scalar_tensor_tensor(qv[:, 1, :], bvec[:, 1, :], -1.0, rnorm[:], ALU.mult, ALU.mult))
            step(dve.tensor_tensor(qv[:, 2, :], bvec[:, 0, :], rnorm[:], ALU.mult))
            dve.wait_ge(dec_ready, 1)
            by = [128, 3, HALF]
            d2 = dec[:].unsqueeze(1).to_broadcast(by)
            step(dve.scalar_tensor_tensor(dq[:], qv[:], 2.0, d2, ALU.mult, ALU.mult))
            dve.wait_ge(sin_ready, 2)
            step(dve.tensor_tensor(wq[:], dq[:], cos_h[:].unsqueeze(1).to_broadcast(by), ALU.mult))
            step(dve.tensor_tensor(qq[:], dq[:], qv[:], ALU.mult))
            step(dve.tensor_tensor(qx[:, 0:2, :], dq[:, 0:2, :], qv[:, 1:3, :], ALU.mult))
            step(dve.tensor_tensor(qx[:, 2, :], dq[:, 0, :], qv[:, 2, :], ALU.mult))
            step(dve.tensor_tensor(bsq[:], d2, qq[:], ALU.subtract))

            def entry(o, c):
                return rmat[:, :, o, c, :].rearrange("p t b -> p b t")

            def by_image(ap):
                return ap.rearrange("p (b t) -> p b t", t=SEQ)

            for o, (a, b) in enumerate(((1, 2), (2, 0), (0, 1))):
                step(dve.tensor_tensor(entry(o, o), by_image(bsq[:, a, :]), by_image(qq[:, b, :]), ALU.subtract))
            for o, c, pair, w, op in ((0, 1, 0, 2, ALU.subtract), (0, 2, 2, 1, ALU.add), (1, 0, 0, 2, ALU.add),
                                      (1, 2, 1, 0, ALU.subtract), (2, 0, 2, 1, ALU.subtract), (2, 1, 1, 0, ALU.add)):
                step(dve.tensor_tensor(entry(o, c), by_image(qx[:, pair, :]), by_image(wq[:, w, :]), op))
            dve.wait_ge(inj_ready, 3)
            step(dve.tensor_copy(hs[:, 0, 0:3, :], rmat[:, 0, :, 3, :]))
            m = [0]

            def scan_link(ins):
                m[0] += 1
                ins.then_inc(scan_step, 1)
                dve.wait_ge(scan_step, m[0])

            for t in range(1, SEQ):
                scan_link(dve.tensor_tensor(prod[:], rmat[:, t], hs[:, t - 1].unsqueeze(1)
                                            .to_broadcast([128, 3, 4, IMAGES // 2]), ALU.mult))
                last = dve.tensor_reduce(hs[:, t, 0:3, :], prod[:].rearrange("p o c b -> p o b c"), AX_X, ALU.add)
                if t < SEQ - 1:
                    scan_link(last)
            last.then_inc(scan_done, 1)
            dve.wait_ge(scan_done, 1)
            dve.wait_ge(hx_ready, NTILES + 1)
            for c in range(3):
                dve.tensor_copy(by_image(hz[64:128, c, HALF:TOKENS]), hs[64:128, :, c, :].rearrange("p t b -> p b t"))\
                   .then_inc(hz_dve, 1)
            layer_norm(3, xw, lambda i: dve.wait_ge(ht_ready, i + 1))
            dve.wait_ge(base2_ready, NTILES)
            for i, r in enumerate(ROWS):
                dve.wait_ge(ln[3]["xn"], i + 1)
                dve.tensor_tensor(xw[0:r, i, :], xw[0:r, i, :], p2("gamma", r), ALU.mult).then_inc(t_ready, 1)
            for i, r in enumerate(ROWS):
                dve.wait_ge(t_ready, NTILES + i + 1)
                dve.tensor_tensor(h[0:r, i, :], h[0:r, i, :], xw[0:r, i, :], ALU.add).then_inc(h3_ready, 1)
            layer_norm(4, h, lambda i: dve.wait_ge(h3_ready, i + 1))
            evac_transposed(4, 5, 128)
            split_x(1)
            route(1, E1, 1, True)
            dve.wait_ge(rt[1]["comb"], 1)

            def period1(p, k, pair, age, has_up, has_next):
                s = moe[1]
                for j in range(C1):
                    if has_up:
                        dve.wait_ge(s["hid_hi"], C1 * p + j + 1)
                        if j == 0 and age > 1:
                            dve.wait_ge(s["down"], NTILES * p - NTILES)
                        slot = 2 * (j % 3)
                        dve.scalar_tensor_tensor(hid_lo[k][:, j, :].rearrange("p (a b) -> p a b", a=2),
                                                 ps[:, slot:slot + 2, 0:HALF], 0.0,
                                                 hid_hi[k][:, j, :].bitcast(F32).rearrange("p (a b) -> p a b", a=2),
                                                 ALU.max, ALU.subtract).then_inc(s["hid_lo"], 1)
                if age:
                    for i in range(NTILES):
                        add_expert(s, p, k, i, age)

            periods(dve, E1, period1)

        @block.tensor
        def _(pe):
            def transposes(k, src, ready, b0, twice):
                for i, r in enumerate(ROWS):
                    ready(i)
                    b, c = (b0, 128 * i) if i < 4 else (b0 + 2, 0)
                    pe.transpose(ps[:, b, c:c + r], src[0:r, i, 0:128], ident[0:r, 0:r])
                    b, c = (b0 + 1, 128 * i) if i < 4 else (b0 + 2, 128)
                    ins = pe.transpose(ps[0:KB, b, c:c + r], src[0:r, i, 128:DIM], ident[0:r, 0:r])
                    if twice:
                        ins = pe.matmul(ps[KB:128, b, c:c + r], src[0:r, i, 128:DIM], ident[0:r, 0:r], start=True,
                                        stop=True, skip_group_check=True)
                    ins.then_inc(tr[k]["mm"], 1)

            def xt_ready(k):
                pe.wait_ge(tr[k]["act"], 3)
                pe.wait_ge(tr[k]["dve"], 1)

            def group(dst, pairs):
                for n, (a, b) in enumerate(pairs):
                    ins = pe.matmul(dst, a, b, start=(n == 0), stop=(n == len(pairs) - 1), skip_group_check=True)
                return ins

            pe.wait_ge(tokw_in, 16)
            pe.wait_ge(rows_in, 16)
            for i, r in enumerate(ROWS):
                pe.wait_ge(xp_in[i], 16)
                a = PIXC * TILE * i
                group(ps[0:r, i, 0:DIM], [(xp_sb[:, a + c * r:a + (c + 1) * r], tokw_sb[:, c, :]) for c in range(PIXC)]
                      + [(rw("ind", 2)[:, tile_cols(i)], rw("tokb", 2))]).then_inc(tok_mm, 1)
            pe.wait_ge(ident_in, 16)
            transposes(0, xn, lambda i: pe.wait_ge(ln[0]["xn"], i + 1), 5, False)

            xt_ready(0)
            pe.wait_ge(pk1_in, 16)
            for n, (c, which) in enumerate(((0, 0), (0, 1), (1, 0), (1, 1))):
                K = (KA, KB)[c]
                w0_ = which * DIM + c * 128
                for kc, (name, kk) in enumerate((("wqkv_a", KA), ("wqkv_b", KB))):
                    for hh in range(2):
                        ins = pe.matmul(ps[0:K, 2 * n + hh, 0:HALF], p1(name, kk)[:, w0_:w0_ + K],
                                        xt[0:kk, kc, hh * HALF:(hh + 1) * HALF], start=(kc == 0), stop=(kc == 1),
                                        skip_group_check=True)
                ins.then_inc(qk_mm, 1)
            for i, r in enumerate(ROWS):
                pe.wait_ge(q_ready, (1, 1, 1, 1, 2)[i])
                pe.wait_ge(k_ready, (0, 0, 1, 1, 1)[i]) if i >= 2 else None
                group(ps[0:r, i, 0:DIM], [
                    (rw("ones")[:, 0:r], rw("bv")),
                    (xt[0:KA, 0, tile_cols(i)], p1("wqkv_a")[:, 2 * DIM:3 * DIM]),
                    (xt[0:KB, 1, tile_cols(i)], p1("wqkv_b", KB)[:, 2 * DIM:3 * DIM])]).then_inc(v_mm, 1)
            pe.wait_ge(v_ready, 4)
            pe.wait_ge(k_ready, 2)
            for n in range(4):
                hf, ih = n // 2, n % 2
                if ih == 0:
                    pe.wait_ge(qg_dve, (HG, 3 * HG)[hf])
                    pe.wait_ge(qg_act, HG)
                for b in range(IMAGES // 2):
                    img = ih * (IMAGES // 2) + b
                    ins = group(ps[0:HROWS, n, b * SEQ:(b + 1) * SEQ], [
                        (qg[0:kk, kc, img, hf * HROWS:(hf + 1) * HROWS], k_sb[0:kk, kc, img * SEQ:(img + 1) * SEQ])
                        for kc, kk in ((0, KA), (1, KB))])
                ins.then_inc(sc_mm, 1)
            pe.wait_ge(wmix_ready, 1)
            pe.wait_ge(v_ready, NTILES)

            def mix(i):
                r = ROWS[i]
                pe.wait_ge(prob_ready, 4)
                if i >= 2:
                    pe.wait_ge(abd_ready, i - 1)
                pairs = [(rw("ones")[:, 0:r], rw("bw"))]
                for hf in range(2):
                    both = prob[0:HROWS, 2 * hf:2 * hf + 2, :].rearrange("p a b -> p (a b)")
                    pairs.append((both[:, tile_cols(i)], wmix[0:HROWS, hf].rearrange("p g n -> p (g n)")))
                group(ps[0:r, 4 + i % 2, 0:HEADS * SEQ], pairs).then_inc(mix_mm, 1)

            def attend(i):
                r = ROWS[i]
                pe.wait_ge(abd_ready, i + 1)
                if i >= 2:
                    pe.wait_ge(o_ready, i - 1)
                for g in range(HEADS):
                    ins = pe.matmul(ps[0:r, 6 + i % 2, g * HDIM:(g + 1) * HDIM], abd[i % 2][0:r, g, 0:r],
                                    v_sb[0:r, i, g * HDIM:(g + 1) * HDIM], start=True, stop=True, skip_group_check=True)
                ins.then_inc(av_mm, 1)

            mix(0)
            for i in range(NTILES):
                if i + 1 < NTILES:
                    mix(i + 1)
                attend(i)
            transposes(1, xw, lambda i: pe.wait_ge(o_ready, i + 1), 0, False)
            xt_ready(1)
            for i, r in enumerate(ROWS):
                group(ps[0:r, 3 + i, 0:DIM], [
                    (rw("ones")[:, 0:r], rw("bp")),
                    (xt[0:KA, 0, tile_cols(i)], p1("wp_a")),
                    (xt[0:KB, 1, tile_cols(i)], p1("wp_b", KB))]).then_inc(proj_mm, 1)

            transposes(2, xw, lambda i: pe.wait_ge(t_ready, i + 1), 0, True)
            xt_ready(2)
            pe.wait_ge(pk2_in, 16)
            pe.wait_ge(h1_ready, NTILES)
            for i, r in enumerate(ROWS):
                group(ps[0:r, 6, i * E0:(i + 1) * E0], [
                    (rw("ones")[:, 0:r], rw("gb")),
                    (xt[0:KA, 0, tile_cols(i)], p2("gate_a")),
                    (xt[0:KB, 1, tile_cols(i)], p2("gate_b", KB))]).then_inc(rt[0]["mm"], 1)

            def up(layer, p, k, first):
                s = layer["s"]
                pe.wait_ge(s["w1_hi"], 2 * p + 2)
                pe.wait_ge(s["w1_lo"], 2 * p + 2)
                hi, lo = w1_hi[k], w1_lo[k]
                for j in range(6):
                    if layer is LAYERS[0]:
                        col = (j // 2 + C0 * (j % 2)) * 128
                        if j in (1, 3, 5) and not (first and j < 3):
                            pe.wait_ge(s["glu"], C0 * p + (0, 1, 2)[j // 2])
                        elif j in (0, 2, 4) and not (first and j < 3):
                            pe.wait_ge(s["lin"], C0 * p + (-1, 0, 1)[j // 2])
                    else:
                        col = j * 128
                        if not (first and j < 3):
                            pe.wait_ge(s["hid_lo"], C1 * p + j - 2)
                    slot = 2 * (j % 3)
                    a, b = slice(col, col + 128), slice(W1C + col, W1C + col + 128)
                    parts = [(hi[:, a], xa_hi[:]), (hi[:, b], xb_hl[:]), (hi[:, a], xa_lo[:]), (lo[:, a], xa_hi[:]),
                             (lo[0:KB, b], xb_hl[0:KB, :])]
                    for n, (w, x) in enumerate(parts):
                        for hh in range(2):
                            ins = pe.matmul(ps[:, slot + hh, 0:HALF], w, x[:, hh * HALF:(hh + 1) * HALF], start=(n == 0),
                                            stop=(n == len(parts) - 1), skip_group_check=True)
                    ins.then_inc(s["up"], 1)

            def down(layer, p, k, age):
                s, C, b = layer["s"], layer["C"], 1 - k
                pe.wait_ge(s["hid_lo"], C * p)
                pe.wait_ge(s["w2_hi"], p)
                pe.wait_ge(s["w2_lo"], p)
                for i, r in enumerate(ROWS):
                    if age > 1 or i > 1:
                        pe.wait_ge(s["y"], NTILES * p - NTILES + max(i - 1, 0))
                    pairs = []
                    for c in range(C):
                        w = slice(c * DIM, (c + 1) * DIM)
                        pairs += [(hid_hi[b][:, c, tile_cols(i)], w2_hi[b][:, w]), (hid_hi[b][:, c, tile_cols(i)], w2_lo[b][:, w]),
                                  (hid_lo[b][:, c, tile_cols(i)], w2_hi[b][:, w])]
                    group(ps[0:r, 6 + (NTILES * b + i) % 2, 0:DIM], pairs).then_inc(s["down"], 1)

            def x_split(k):
                pe.wait_ge(xhi[k], 3)
                pe.wait_ge(xlo[k], 2)

            def make_period(layer, after_first):
                def period(p, k, pair, age, has_up, has_next):
                    if has_up:
                        up(layer, p, k, age == 0)
                    if age == 0:
                        after_first()
                    else:
                        down(layer, p, k, age)
                return period

            def bias_rows():
                pe.wait_ge(rt[0]["comb"], 1)
                for i, r in enumerate(ROWS):
                    b, c = (7, 128 * i) if i < 4 else (6, 0)
                    pe.transpose(ps[0:E0, b, c:c + r], comb[0:r, i, :], ident[0:r, 0:r]).then_inc(ct_mm, 1)
                pe.wait_ge(ct_ready, 2)
                for i, r in enumerate(ROWS):
                    if i >= 2:
                        pe.wait_ge(base_ready, i - 1)
                    pe.matmul(ps[0:r, 6 + i % 2, 0:DIM], comb_t[:, i, 0:r], rw("b2", E0), start=True, stop=True)\
                      .then_inc(b2_mm, 1)
                pe.wait_ge(base_ready, NTILES)

            x_split(0)
            periods(pe, E0, make_period(LAYERS[0], bias_rows))

            transposes(3, xn, lambda i: pe.wait_ge(ln[2]["xn"], i + 1), 5, False)
            xt_ready(3)
            for n in (0, 1, 2, 6, 3, 4, 5):
                for kc, (name, kk) in enumerate((("wall_a", KA), ("wall_b", KB))):
                    for hh in range(2):
                        ins = pe.matmul(ps[hh * 64:(hh + 1) * 64, n, 0:HALF], p2(name, kk)[:, n * NBLK:(n + 1) * NBLK],
                                        xt[0:kk, kc, hh * HALF:(hh + 1) * HALF], start=(kc == 0), stop=(kc == 1),
                                        skip_group_check=True)
                ins.then_inc(wall_mm, 1)
            pe.wait_ge(hz_act, 3)
            pe.wait_ge(hz_dve, 3)
            pe.wait_ge(hx_ready, NTILES + 1)
            pe.wait_ge(inj_ready, 3)
            for i, r in enumerate(ROWS):
                for c in range(3):
                    ins = pe.matmul(ps[0:r, i, c * NBLK:(c + 1) * NBLK], hz[:, c, tile_cols(i)], p2("sel"), start=True,
                                    stop=True, skip_group_check=True)
                ins.then_inc(ht_mm, 1)
            transposes(4, xn, lambda i: pe.wait_ge(ln[4]["xn"], i + 1), 5, True)
            xt_ready(4)
            for i, r in enumerate(ROWS):
                group(ps[0:r, 6, i * E1:(i + 1) * E1], [
                    (xt[0:KA, 0, tile_cols(i)], p2("rout_a")),
                    (xt[0:KB, 1, tile_cols(i)], p2("rout_b", KB))]).then_inc(rt[1]["mm"], 1)
            x_split(1)

            def combined():
                pe.wait_ge(rt[1]["comb"], 1)

            periods(pe, E1, make_period(LAYERS[1], combined))


def lay_out(a):
    import numpy as np

    def ab(w):
        second = np.zeros((128, w.shape[1]), w.dtype)
        second[0:KB] = w[KA:DIM]
        return w[0:KA], second

    def pack(where, cols, parts, n=128):
        out = np.zeros((n, cols), np.float32)
        for name, (at, width) in where.items():
            p = parts[name]
            out[0:p.shape[0], at:at + width] = p
        return out

    x = a["x"].reshape(IMAGES, 3, 4, 16, 4, 16).transpose(1, 3, 5, 0, 2, 4).reshape(PIX, IMAGES, PATCHES)
    cols = np.zeros((PIX, IMAGES, SEQ), x.dtype)
    cols[:, :, 1:] = x
    cols = cols.reshape(PIXC, 128, TOKENS).transpose(1, 0, 2)
    xp = np.concatenate([cols[:, :, TILE * i:TILE * i + r].reshape(128, PIXC * r) for i, r in enumerate(ROWS)], axis=1)
    tokw = a["L0_tok_W"].T.reshape(PIXC, 128, DIM).transpose(1, 0, 2).reshape(128, PIXC * DIM)

    ind = np.zeros((2, IMAGES, SEQ), np.float32)
    ind[0, :, 1:] = 1.0
    ind[1, :, 0] = 1.0
    bqkv = a["L0_attn_b_qkv"]
    rows = pack(RW, RW_COLS, {
        "ind": ind.reshape(2, TOKENS), "tokb": np.stack([a["L0_tok_b"], a["cls_tok"].reshape(DIM)]),
        "ones": np.ones((1, 128), np.float32), "bv": bqkv[None, 2 * DIM:], "bp": a["L0_attn_b_proj"][None],
        "bw": np.repeat(a["L0_attn_b_w"], SEQ)[None], "gb": a["L0_ffn_gate_b"][None], "b2": a["L0_ffn_mlp2_b"]}, 16)

    wqkv_a, wqkv_b = ab(a["L0_attn_w_qkv"])
    wp_a, wp_b = ab(a["L0_attn_w_proj"])
    wl_a, wl_b = ab(np.repeat(a["L0_attn_w_l"], HDIM, axis=0))
    bq_a, bq_b = ab(bqkv[0:DIM, None])
    bk_a, bk_b = ab(bqkv[DIM:2 * DIM, None])
    ww = np.repeat(a["L0_attn_w_w"].reshape(2, HG, HEADS), SEQ, axis=1)
    at = np.arange(HROWS)
    pk1 = pack(PK1, PK1_COLS, {
        "ident": np.eye(128, dtype=np.float32), "wqkv_a": wqkv_a, "wqkv_b": wqkv_b,
        "bqk": np.concatenate([bq_a, bq_b, bk_a, bk_b], axis=1), "wl": np.concatenate([wl_a, wl_b], axis=1),
        "bl": np.repeat(a["L0_attn_b_l"].reshape(2, HG), SEQ, axis=1).T, "ww": np.concatenate([ww[0], ww[1]], axis=1),
        "delta": (at[:, None] % SEQ == np.arange(SEQ)).astype(np.float32),
        "mask": (np.arange(TILE)[:, None] // SEQ == np.arange(IMG_TILE)).astype(np.float32),
        "wp_a": wp_a, "wp_b": wp_b})

    def comps(w):
        return w.reshape(-1, NBLK, 3).transpose(0, 2, 1).reshape(-1, DIM)

    wall = np.concatenate([comps(a["L1_attn_Wb"]), comps(a["L1_attn_Wi"]), np.repeat(a["L1_attn_Wd"], NBLK, axis=1)], axis=1)
    ball = np.concatenate([comps(a["L1_attn_bb"]), comps(a["L1_attn_bi"]), np.repeat(a["L1_attn_bd"], NBLK)[None]], axis=1)
    ball = ball.reshape(7, NBLK).T
    wall_a, wall_b = ab(wall)
    gate_a, gate_b = ab(a["L0_ffn_gate_w"].T)
    rout_a, rout_b = ab(a["L1_ffn_router_w"])
    b1 = a["L0_ffn_mlp1_b"].reshape(E0, F0, 2).transpose(0, 2, 1).reshape(E0 * 6, 128).T

    def tri(n):
        return np.broadcast_to(np.tril(np.ones((n, n), np.float32), -1).reshape(1, n * n), (128, n * n))

    def every_row(v):
        return np.broadcast_to(v[None], (128, DIM))

    pk2 = pack(PK2, PK2_COLS, {
        "scale": every_row(a["L0_ffn_norm_scale"]), "gamma": every_row(a["L1_attn_gamma"]), "beta": every_row(a["L1_attn_beta"]),
        "gate_a": gate_a, "gate_b": gate_b, "b1": b1, "tri0": tri(E0), "tri1": tri(E1), "wall_a": wall_a, "wall_b": wall_b,
        "ball": np.concatenate([ball, ball]), "sel": np.concatenate([np.eye(NBLK, dtype=np.float32)] * 2),
        "rout_a": rout_a, "rout_b": rout_b})

    def expert_blocks(first, second):
        E, C = first.shape[0], second.shape[1] // 128
        tail = first[:, KA:DIM]
        second = second.reshape(E, C, 128, DIM).transpose(0, 2, 1, 3).reshape(E, 128, C * DIM)
        return np.concatenate([first[:, 0:KA], np.concatenate([tail, tail], axis=1), second], axis=2)

    m1 = a["L0_ffn_mlp1_w"].reshape(E0, F0, 2, DIM).transpose(0, 3, 2, 1).reshape(E0, DIM, 2 * F0)
    w0 = expert_blocks(m1, a["L0_ffn_mlp2_w"].transpose(0, 2, 1))
    w1 = expert_blocks(a["L1_ffn_wi"], a["L1_ffn_wo"])
    return {"xp": xp, "tokw": tokw, "rows": rows, "pk1": pk1, "pk2": pk2, "w0": w0, "w1": w1}


def kernel(**inputs):
    import numpy as np
    import concourse.bacc as bacc
    from concourse.bass_utils import run_bass_kernel_spmd

    nc = bacc.Bacc("TRN2", target_bir_lowering=False, num_devices=1)
    arrays, args = {}, []
    for name, v in lay_out({k: np.asarray(v) for k, v in inputs.items()}).items():
        v = np.ascontiguousarray(v)
        arrays[f"in_{name}"] = v
        args.append(nc.dram_tensor(f"in_{name}", v.shape, mybir.dt.from_np(v.dtype), kind="ExternalInput").ap())
    args.append(nc.dram_tensor("out_rows", (TOKENS, DIM), F32, kind="ExternalOutput").ap())
    build(nc, *args)
    r = run_bass_kernel_spmd(nc, [arrays], core_ids=[0])
    return r.results[0]["out_rows"].reshape(IMAGES, SEQ, DIM)
```

```python
from contextlib import ExitStack

import concourse.bass as bass
from concourse import mybir

F32 = mybir.dt.float32
F32R = mybir.dt.float32r
ALU = mybir.AluOpType
ACT = mybir.ActivationFunctionType
AX_X = mybir.AxisListType.X

IMAGES, PATCHES, DIM = 32, 16, 192
SEQ = PATCHES + 1
TOKENS = IMAGES * SEQ
IMG_TILE = 7
TILE = IMG_TILE * SEQ
NTILES = -(-IMAGES // IMG_TILE)
TILE_IMGS = [min(IMG_TILE, IMAGES - IMG_TILE * i) for i in range(NTILES)]
ROWS = [n * SEQ for n in TILE_IMGS]
HALF = TOKENS // 2
KA, KB = 128, DIM - 128
PIX = 768
PIXC = PIX // 128
HEADS, HDIM = 12, 16
HG = HEADS // 2
HROWS = HG * SEQ
HD = HG * HDIM
E0, F0, TOPK = 16, 384, 4
E1, F1 = 8, 768
C0, C1 = F0 // 128, F1 // 128
W1C = 768
W2C0, W2C1 = C0 * DIM, C1 * DIM
NBLK = DIM // 3
LIMIT = 7.0
EPS = 1e-5
PI = 3.14159265358979
TWO_PI_HI = 6.28125
TWO_PI_LO = 2 * PI - TWO_PI_HI
MAGIC = 12582912.0


def layout(blocks):
    at, out = 0, {}
    for name, n in blocks:
        out[name] = (at, n)
        at += n
    return out, at


PK1, PK1_COLS = layout([
    ("ident", 128), ("wqkv_a", 3 * DIM), ("wqkv_b", 3 * DIM), ("bqk", 4), ("wl", 2 * HEADS), ("bl", 2), ("head", HG),
    ("ww", 2 * HEADS), ("delta", SEQ), ("mask", IMG_TILE), ("wp_a", DIM), ("wp_b", DIM), ("bp", DIM)])
PK2, PK2_COLS = layout([
    ("scale", DIM), ("gate_a", E0), ("gate_b", E0), ("gb", E0), ("b1", E0 * 6),
    ("wall_a", 7 * NBLK), ("wall_b", 7 * NBLK), ("ball", 7), ("gamma", DIM), ("beta", DIM),
    ("sel", NBLK), ("rout_a", E1), ("rout_b", E1)])
RW, RW_COLS = layout([
    ("ones", 128), ("bv", DIM), ("bw", HEADS * SEQ), ("b2", DIM)])


def build(nc, xp, tokw, rows, pk1, pk2, w0, w1, out):
    ctx = ExitStack()
    with ctx:
        def sb(name, shape, dt=F32, stack=ctx):
            return stack.enter_context(nc.sbuf_tensor(name, shape, dt))

        def sem(name):
            return ctx.enter_context(nc.semaphore(name))

        pk2_sb = sb("pk2_sb", [128, PK2_COLS])
        rows_sb = sb("rows_sb", [16, RW_COLS])
        ident = sb("ident", [128, 128])
        h = sb("h", [128, NTILES, DIM])
        xn = sb("xn", [128, NTILES, DIM])
        xw = sb("xw", [128, NTILES, DIM])
        xt = sb("xt", [128, 2, TOKENS])
        stats = sb("stats", [128, NTILES, 6])
        mv = sb("mv", [128, NTILES, 2])
        sd = sb("sd", [128, NTILES])
        rstd = sb("rstd", [128, NTILES])
        squares = sb("squares", [128, 2, NTILES])
        roots = sb("roots", [128, 2, NTILES])
        rroots = sb("rroots", [128, 2, NTILES])
        gl = sb("gl", [128, NTILES, E0])
        gmax = sb("gmax", [128, NTILES])
        gsum = sb("gsum", [128, NTILES])
        grec = sb("grec", [128, NTILES])
        gexp = sb("gexp", [128, NTILES, E0])
        top8 = sb("top8", [128, NTILES, 8])
        above = sb("above", [128, NTILES, E0])
        equal = sb("equal", [128, NTILES, E0])
        same = [sb(f"same{k}", [128, NTILES, E0]) for k in range(2)]
        count = sb("count", [128, NTILES])
        comb = sb("comb", [128, NTILES, E0])
        eps_t = sb("eps_t", [128, 1])
        hpi_t = sb("hpi_t", [128, 1])
        eps_col, half_pi_col = eps_t[:, 0:1], hpi_t[:, 0:1]
        comb_t = sb("comb_t", [16, NTILES, 128])
        b1x = sb("b1x", [128, E0 * 6])

        xa_hi = sb("xa_hi", [128, TOKENS], F32R)
        xa_lo = sb("xa_lo", [128, TOKENS], F32R)
        xb_hi = sb("xb_hi", [128, TOKENS], F32R)
        xb_hl = sb("xb_hl", [128, TOKENS], F32R)
        raw1 = [sb(f"raw1_{k}", [128, 2 * W1C]) for k in range(2)]
        raw2 = [sb(f"raw2_{k}", [128, W2C1]) for k in range(2)]
        w1_hi = [sb(f"w1_hi{k}", [128, 2 * W1C], F32R) for k in range(2)]
        w1_lo = [sb(f"w1_lo{k}", [128, 2 * W1C], F32R) for k in range(2)]

        early = ExitStack()
        pk1_sb = sb("pk1_sb", [128, PK1_COLS], stack=early)
        xp_sb = sb("xp_sb", [128, PIXC * TOKENS], stack=early)
        tokw_sb = sb("tokw_sb", [128, PIXC + 1, DIM], stack=early)
        q_sb = sb("q_sb", [128, 2, TOKENS], stack=early)
        k_sb = sb("k_sb", [128, 2, TOKENS], stack=early)
        v_pad = sb("v_pad", [128, NTILES, HEADS, 32], stack=early)
        sco = sb("sco", [128, 4, HALF], stack=early)
        lg = sb("lg", [128, 4, HALF], stack=early)
        prob = sb("prob", [128, 4, HALF], stack=early)
        smax = sb("smax", [128, 4, IMAGES // 2], stack=early)
        ssum = sb("ssum", [128, 4, IMAGES // 2], stack=early)
        srec = sb("srec", [128, 4, IMAGES // 2], stack=early)
        lmix = sb("lmix", [128, 2, HG * 2, SEQ], stack=early)
        wmix = sb("wmix", [128, 2, HG * 2, SEQ], stack=early)
        abd = [sb(f"abd{k}", [128, HEADS, TILE], stack=early) for k in range(2)]
        qd = sb("qd", [128, 2, IMAGES, HROWS], stack=early)
        early.close()
        scan = ExitStack()
        bvec = sb("bvec", [128, 3, HALF], stack=scan)
        bsq = sb("bsq", [128, 3, HALF], stack=scan)
        bun = sb("bun", [128, 3, HALF], stack=scan)
        qv = sb("qv", [128, 3, HALF], stack=scan)
        dq = sb("dq", [128, 3, HALF], stack=scan)
        wq = sb("wq", [128, 3, HALF], stack=scan)
        qq = sb("qq", [128, 3, HALF], stack=scan)
        qx = sb("qx", [128, 3, HALF], stack=scan)
        dec = sb("dec", [128, HALF], stack=scan)
        norm = sb("norm", [128, HALF], stack=scan)
        rnorm = sb("rnorm", [128, HALF], stack=scan)
        half_ang = sb("half_ang", [128, HALF], stack=scan)
        turns = sb("turns", [128, HALF], stack=scan)
        habs = sb("habs", [128, HALF], stack=scan)
        sin_h = sb("sin_h", [128, HALF], stack=scan)
        cos_h = sb("cos_h", [128, HALF], stack=scan)
        rmat = sb("rmat", [128, SEQ, 3, 4, IMAGES // 2], stack=scan)
        hs = sb("hs", [128, SEQ, 4, IMAGES // 2], stack=scan)
        prod = sb("prod", [128, 3, 4, IMAGES // 2], stack=scan)
        hz = sb("hz", [128, 3, TOKENS], stack=scan)
        scan.close()
        hid_hi = [sb(f"hid_hi{k}", [128, C1, TOKENS], F32R) for k in range(2)]
        hid_lo = [sb(f"hid_lo{k}", [128, C1, TOKENS], F32R) for k in range(2)]
        w2_hi = [sb(f"w2_hi{k}", [128, W2C1], F32R) for k in range(2)]
        w2_lo = [sb(f"w2_lo{k}", [128, W2C1], F32R) for k in range(2)]
        lin = sb("lin", [128, C0, TOKENS])
        glu = sb("glu", [128, C0, TOKENS])
        gact = sb("gact", [128, C0, TOKENS])
        aval = sb("aval", [128, C0, TOKENS])

        ps = ctx.enter_context(nc.psum_tensor("ps", [128, 8, 512], F32))

        def p1(name, r=128):
            a, n = PK1[name]
            return pk1_sb[0:r, a:a + n]

        def p2(name, r=128):
            a, n = PK2[name]
            return pk2_sb[0:r, a:a + n]

        def rw(name, r=1):
            a, n = RW[name]
            return rows_sb[0:r, a:a + n]

        def tile_cols(i):
            return slice(TILE * i, TILE * i + ROWS[i])

        tokw_in, rows_in, pk1_in, pk2_in, ident_in = (sem(n) for n in ("tokw_in", "rows_in", "pk1_in", "pk2_in", "ident_in"))
        xp_in = [sem(f"xp_in{i}") for i in range(NTILES)]
        cleared = sem("cleared")
        tok_mm, h0_ready = sem("tok_mm"), sem("h0_ready")
        ln = [dict(step=sem(f"ln{k}_step"), mean=sem(f"ln{k}_mean"), sd=sem(f"ln{k}_sd"),
                   xn=sem(f"ln{k}_xn")) for k in range(5)]
        tr = [dict(mm=sem(f"tr{k}_mm"), act=sem(f"tr{k}_act"), dve=sem(f"tr{k}_dve")) for k in range(5)]
        qk_mm, q_ready, k_ready, v_mm, v_ready = (sem(n) for n in ("qk_mm", "q_ready", "k_ready", "v_mm", "v_ready"))
        qd_ready, sc_mm, sco_ready, lmix_ready, lg_mm, lg_ready = (sem(n) for n in (
            "qd_ready", "sc_mm", "sco_ready", "lmix_ready", "lg_mm", "lg_ready"))
        smax_ready, lg_shift, exp_ready, ssum_ready, srec_ready, prob_ready = (
            sem(n) for n in ("smax_ready", "lg_shift", "exp_ready", "ssum_ready", "srec_ready", "prob_ready"))
        wmix_ready, mix_mm, abd_ready, proj_mm, h1_ready = (
            sem(n) for n in ("wmix_ready", "mix_mm", "abd_ready", "proj_mm", "h1_ready"))
        ssq_ready, rms_sd, rms_rs, t_ready = (sem(n) for n in ("ssq_ready", "rms_sd", "rms_rs", "t_ready"))
        xhi = [sem(f"xhi{k}") for k in range(2)]
        xlo = [sem(f"xlo{k}") for k in range(2)]
        xhl = [sem(f"xhl{k}") for k in range(2)]
        rt = [dict(mm=sem(f"rt{k}_mm"), step=sem(f"rt{k}_step"), shift=sem(f"rt{k}_shift"), exp=sem(f"rt{k}_exp"),
                   comb=sem(f"rt{k}_comb")) for k in range(2)]
        b1_ready, hx_ready, hb_ready, bw_in = (sem(n) for n in ("b1_ready", "hx_ready", "hb_ready", "bw_in"))
        ct_mm, ct_ready, b2_mm, base_ready = (sem(n) for n in ("ct_mm", "ct_ready", "b2_mm", "base_ready"))
        moe = [dict(raw1=[sem(f"m{k}_raw1_{j}") for j in range(2)], raw2=[sem(f"m{k}_raw2_{j}") for j in range(2)],
                    **{n: sem(f"m{k}_{n}") for n in ("w1_hi", "w1_lo", "w2_hi", "w2_lo", "up", "glu", "lin", "clamp",
                                                     "gact", "aval", "hid_hi", "hid_lo", "down", "y")})
               for k in range(2)]
        wall_mm, bvec_ready, dec_ready, inj_ready = (sem(n) for n in ("wall_mm", "bvec_ready", "dec_ready", "inj_ready"))
        nsq_ready, norm_ready, ang_ready, sin_ready, rot_step, wq_ready = (
            sem(n) for n in ("nsq_ready", "norm_ready", "ang_ready", "sin_ready", "rot_step", "wq_ready"))
        scan_step = [sem(f"scan_step{k}") for k in range(2)]
        base2_ready, hz_act, hz_dve, ht_mm, ht_ready, h3_ready = (
            sem(n) for n in ("base2_ready", "hz_act", "hz_dve", "ht_mm", "ht_ready", "h3_ready"))
        stored = sem("stored")

        DOWN_BANKS = (0, 1, 2, 6, 7)
        BIAS_BANKS = (5, 3, 4, 5, 3)

        QUARTERS = (0, 2, 1, 3)

        CLEARED = 7
        DQ_STEP = 15

        LAYERS = [
            dict(E=E0, C=C0, W2=W2C0, dram=w0, s=moe[0]),
            dict(E=E1, C=C1, W2=W2C1, dram=w1, s=moe[1]),
        ]

        def periods(eng, n_experts, period):
            period(0, 0, 0, 0, True, True)
            period(1, 1, 0, 1, True, True)
            with eng.Fori(0, n_experts // 2 - 2) as i:
                period(2 * i + 2, 0, i + 1, 2, True, True)
                period(2 * i + 3, 1, i + 1, 2, True, True)
            period(n_experts - 2, 0, n_experts // 2 - 1, 2, True, False)
            period(n_experts - 1, 1, n_experts // 2 - 1, 2, True, False)
            period(n_experts, 0, n_experts // 2, 2, False, False)

        block = ctx.enter_context(nc.Block())

        @block.sync
        def _(sp):
            sp.dma_start(tokw_sb[:], tokw.rearrange("p (c d) -> p c d", d=DIM)).then_inc(tokw_in, 16)
            for i in range(NTILES):
                cols = slice(PIXC * TILE * i, PIXC * (TILE * i + ROWS[i]))
                sp.dma_start(xp_sb[:, cols], xp[:, cols]).then_inc(xp_in[i], 16)
            sp.dma_start(pk1_sb[:], pk1).then_inc(pk1_in, 16)
            sp.dma_start(rows_sb[:], rows).then_inc(rows_in, 16)
            sp.dma_start(wmix[HROWS:HROWS + 1, 0].rearrange("p g n -> p (g n)"),
                         rows[0:1, RW["bw"][0]:RW["bw"][0] + HEADS * SEQ]).then_inc(bw_in, 16)
            sp.dma_start(pk2_sb[:], pk2).then_inc(pk2_in, 16)

            def load1(layer, dram, e, k):
                sp.dma_start(raw1[k][:], dram[bass.ds(e, 1), :, 0:2 * W1C].rearrange("a p c -> (a p) c"))\
                  .then_inc(layer["s"]["raw1"][k], 16)

            def load2(layer, dram, e, k):
                n = layer["W2"]
                sp.dma_start(raw2[k][:, 0:n], dram[bass.ds(e, 1), :, 2 * W1C:2 * W1C + n].rearrange("a p c -> (a p) c"))\
                  .then_inc(layer["s"]["raw2"][k], 16)

            for n, layer in enumerate(LAYERS):
                s = layer["s"]
                for k in range(2):
                    if n:
                        sp.wait_ge(LAYERS[0]["s"]["w1_hi"], 2 * (E0 - 1 + k))
                        sp.wait_ge(LAYERS[0]["s"]["w1_lo"], 2 * (E0 - 1 + k))
                    load1(layer, layer["dram"], k, k)
                    if n:
                        sp.wait_ge(LAYERS[0]["s"]["w2_hi"], E0 - 1 + k)
                        sp.wait_ge(LAYERS[0]["s"]["w2_lo"], E0 - 1 + k)
                    load2(layer, layer["dram"], k, k)
                with sp.Fori(0, layer["E"] // 2 - 1) as i:
                    for k in range(2):
                        sp.wait_ge(s["w1_hi"], 4 * i + 2 * k + 2)
                        sp.wait_ge(s["w1_lo"], 4 * i + 2 * k + 2)
                        load1(layer, layer["dram"], 2 * i + 2 + k, k)
                        sp.wait_ge(s["w2_hi"], 2 * i + k + 1)
                        sp.wait_ge(s["w2_lo"], 2 * i + k + 1)
                        load2(layer, layer["dram"], 2 * i + 2 + k, k)
            for i in range(NTILES):
                sp.wait_ge(moe[1]["y"], NTILES * (E1 - 1) + i + 1)
                sp.dma_start(out[tile_cols(i), :], h[0:ROWS[i], i, :]).then_inc(stored, 16)
            sp.wait_ge(stored, 16 * NTILES)

        @block.scalar
        def _(act):
            act.dma_start(ident[:], pk1[:, 0:128]).then_inc(ident_in, 16)

            def root(k):
                act.wait_ge(ln[k]["mean"], NTILES)
                act.wait_ge(cleared, CLEARED)
                act.activation(sd[:], mv[:, :, 1], ACT.Sqrt, bias=eps_col).then_inc(ln[k]["sd"], 1)

            def evac_transposed(k, b0, n=KB):
                act.wait_ge(tr[k]["mm"], NTILES)
                act.activation(xt[:, 0, 0:4 * TILE].rearrange("p (t c) -> p t c", t=4),
                               ps[:, b0, :].rearrange("p (t c) -> p t c", t=4)[:, :, 0:TILE], ACT.Copy)\
                   .then_inc(tr[k]["act"], 1)
                act.activation(xt[:, 0, 4 * TILE:TOKENS], ps[:, b0 + 2, 0:ROWS[4]], ACT.Copy).then_inc(tr[k]["act"], 1)
                act.activation(xt[0:n, 1, 4 * TILE:TOKENS], ps[0:n, b0 + 2, 128:128 + ROWS[4]], ACT.Copy)\
                   .then_inc(tr[k]["act"], 1)

            def split_x(k, t):
                act.wait_ge(tr[t]["act"], 3)
                act.wait_ge(tr[t]["dve"], 1)
                act.activation(xa_hi[:], xt[:, 0, :], ACT.Copy).then_inc(xhi[k], 1)
                act.activation(xb_hi[:], xt[:, 1, :], ACT.Copy).then_inc(xhi[k], 1)
                act.activation(xb_hl[0:64, :], xt[0:64, 1, :], ACT.Copy).then_inc(xhi[k], 1)

            def split_w1(layer, e, k, pair, reused):
                s = layer["s"]
                act.wait_ge(s["raw1"][k], 16 * pair + 16)
                if reused:
                    act.wait_ge(s["up"], 6 * e - 6)
                for a in (0, W1C):
                    act.activation(w1_hi[k][:, a:a + W1C], raw1[k][:, a:a + W1C], ACT.Copy).then_inc(s["w1_hi"], 1)

            def split_w2(layer, e, k, pair, reused):
                s = layer["s"]
                act.wait_ge(s["raw2"][k], 16 * pair + 16)
                if reused:
                    act.wait_ge(s["down"], NTILES * e - NTILES)
                act.activation(w2_hi[k][:, 0:layer["W2"]], raw2[k][:, 0:layer["W2"]], ACT.Copy).then_inc(s["w2_hi"], 1)

            root(0)
            evac_transposed(0, 5)

            act.wait_ge(pk1_in, 16)
            for c in range(2):
                act.wait_ge(qk_mm, 2 * c + 2)
                act.activation(k_sb[0:HD, c, :].rearrange("p (a b) -> p a b", a=2), ps[0:HD, 4 * c + 2:4 * c + 4, 0:HALF],
                               ACT.Identity, bias=p1("bqk")[0:HD, 2 + c:3 + c]).then_inc(k_ready, 1)
            for i, r in enumerate(ROWS):
                act.wait_ge(v_mm, i + 1)
                act.activation(v_pad[0:r, i].rearrange("p (q o) (k d) -> p q (o k) d", o=2, k=2)[:, :, 0:4:3, :],
                               ps[0:r, i, 0:DIM].rearrange("p (q o d) -> p q o d", o=2, d=HDIM), ACT.Copy).then_inc(v_ready, 1)

            def scores_out(n):
                act.wait_ge(sc_mm, n + 1)
                act.activation(sco[0:HROWS, QUARTERS[n], :], ps[0:HROWS, QUARTERS[n], 0:HALF], ACT.Copy)\
                   .then_inc(sco_ready, 1)

            def mixed_out(n):
                act.wait_ge(lg_mm, n + 1)
                at = QUARTERS[n]
                act.activation(lg[0:HROWS, at, :], ps[0:HROWS, 4 + at, 0:HALF], ACT.Identity,
                               bias=p1("bl")[0:HROWS, at // 2:at // 2 + 1]).then_inc(lg_ready, 1)

            def exp_scores(n):
                act.wait_ge(lg_shift, n + 1)
                act.activation(prob[0:HROWS, QUARTERS[n], :], lg[0:HROWS, QUARTERS[n], :], ACT.Exp).then_inc(exp_ready, 1)

            scores_out(0)
            scores_out(1)
            scores_out(2)
            mixed_out(0)
            mixed_out(1)
            exp_scores(0)
            exp_scores(1)
            scores_out(3)
            mixed_out(2)
            mixed_out(3)
            exp_scores(2)
            exp_scores(3)

            split_w1(LAYERS[0], 0, 0, 0, False)
            split_w1(LAYERS[0], 1, 1, 0, False)

            evac_transposed(1, 0)

            act.wait_ge(ssq_ready, 4)
            act.wait_ge(cleared, CLEARED)
            act.activation(roots[:], squares[:], ACT.Sqrt, bias=eps_col).then_inc(rms_sd, 1)
            evac_transposed(2, 0, 128)
            split_x(0, 2)

            def exps(k, E):
                act.wait_ge(rt[k]["shift"], 1)
                act.activation(gexp[:, :, 0:E], gexp[:, :, 0:E], ACT.Exp).then_inc(rt[k]["exp"], 1)


            def period0(p, k, pair, age, has_up, has_next):
                layer, s = LAYERS[0], moe[0]

                def linear(j):
                    act.wait_ge(s["up"], 6 * p + 2 * j + 2)
                    if age:
                        act.wait_ge(s["aval"], C0 * p - C0 + j + 1)
                    slot = 2 * ((2 * j + 1) % 3)
                    act.activation(lin[:, j, :].rearrange("p (a b) -> p a b", a=2), ps[:, slot:slot + 2, 0:HALF],
                                   ACT.Identity, bias=b1x[:, bass.ds(6 * p + 3 + j, 1)]).then_inc(s["lin"], 1)

                def gated(j):
                    act.wait_ge(s["glu"], C0 * p + j + 1)
                    if age:
                        act.wait_ge(s["aval"], C0 * p - C0 + j + 1)
                    act.activation(gact[:, j, :], glu[:, j, :], ACT.Gelu_apprx_sigmoid).then_inc(s["gact"], 1)

                def high(j, e, b):
                    act.wait_ge(s["aval"], C0 * e + j + 1)
                    if age > 1 and j == 0:
                        act.wait_ge(s["down"], NTILES * p - NTILES)
                    act.activation(hid_hi[b][:, j, :], aval[:, j, :], ACT.Copy).then_inc(s["hid_hi"], 1)

                if has_up:
                    linear(0)
                    gated(0)
                    linear(1)
                    high(0, p, k)
                    gated(1)
                    linear(2)
                    gated(2)
                    high(1, p, k)
                if has_next:
                    split_w1(layer, p + 2, k, pair + 1, True)
                if not has_up:
                    act.wait_ge(ct_mm, NTILES)
                    act.activation(comb_t[:, 0:4, 0:TILE], ps[0:E0, 3, :].rearrange("p (t c) -> p t c", t=4)[:, :, 0:TILE],
                                   ACT.Copy).then_inc(ct_ready, 1)
                    act.activation(comb_t[:, 4, 0:ROWS[4]], ps[0:E0, 4, 0:ROWS[4]], ACT.Copy).then_inc(ct_ready, 1)
                if has_up:
                    split_w2(layer, p, k, pair, age > 1)
                    high(2, p, k)

            exps(0, E0)
            periods(act, E0, period0)

            root(2)
            evac_transposed(3, 5)

            def wall_out(func, dst, n, half):
                bank, a = 2 * (n // 2) + half, 64 * (n % 2)
                act.wait_ge(wall_mm, bank + 1)
                return act.activation(dst, ps[a:a + 64, bank, 0:HALF], func, bias=p2("ball")[a:a + 64, n:n + 1])

            for c in range(3):
                wall_out(ACT.Identity, bvec[0:64, c, :], c, 0).then_inc(bvec_ready, 1)
            act.wait_ge(nsq_ready, 1)
            act.activation(norm[:], norm[:], ACT.Sqrt).then_inc(norm_ready, 1)
            for half in range(2):
                wall_out(ACT.Sigmoid, dec[64 * half:64 * half + 64, :], 3, half).then_inc(dec_ready, 1)
            act.wait_ge(ang_ready, 2)
            act.activation(sin_h[:], half_ang[:], ACT.Sin).then_inc(sin_ready, 1)
            act.activation(cos_h[:], habs[:], ACT.Sin, scale=-1.0, bias=half_pi_col).then_inc(sin_ready, 1)
            halves = "p (b t) -> p b t"
            for half in range(2):
                for c in range(2):
                    bank, a, o = 4 + half, 64 * c, 64 * half
                    act.wait_ge(wall_mm, bank + 1)
                    act.activation(rmat[o:o + 64, :, c, 3, :].rearrange("p t b -> p b t"),
                                   ps[a:a + 64, bank, 0:HALF].rearrange(halves, t=SEQ), ACT.Identity,
                                   bias=p2("ball")[a:a + 64, 4 + c:5 + c]).then_inc(inj_ready, 1)
            act.wait_ge(wall_mm, 8)
            act.activation(rmat[:, :, 2, 3, :].rearrange("p t b -> p b t"), ps[:, 6, 0:HALF].rearrange(halves, t=SEQ),
                           ACT.Identity, bias=p2("ball")[:, 6:7]).then_inc(inj_ready, 1)
            split_w1(LAYERS[1], 0, 0, 0, False)
            split_w1(LAYERS[1], 1, 1, 0, False)
            for chain in range(2):
                act.wait_ge(scan_step[chain], 2 * SEQ - 2)
            act.wait_ge(hx_ready, NTILES + 1)
            for c in range(3):
                act.activation(hz[0:64, c, 0:HALF].rearrange(halves, t=SEQ),
                               hs[0:64, :, c, :].rearrange("p t b -> p b t"), ACT.Copy).then_inc(hz_act, 1)
            for i, r in enumerate(ROWS):
                act.wait_ge(ht_mm, i + 1)
                act.activation(xw[0:r, i, :].rearrange("p (b c) -> p c b", c=3),
                               ps[0:r, i, 0:DIM].rearrange("p (c b) -> p c b", c=3), ACT.Copy).then_inc(ht_ready, 1)
            root(3)
            root(4)
            evac_transposed(4, 5, 128)
            split_x(1, 4)

            def period1(p, k, pair, age, has_up, has_next):
                layer, s = LAYERS[1], moe[1]
                for j in range(C1 if has_up else 0):
                    act.wait_ge(s["up"], 6 * p + j + 1)
                    if j == 0 and age > 1:
                        act.wait_ge(s["down"], NTILES * p - NTILES)
                    slot = 2 * (j % 3)
                    act.activation(hid_hi[k][:, j, :].rearrange("p (a b) -> p a b", a=2), ps[:, slot:slot + 2, 0:HALF],
                                   ACT.Relu).then_inc(s["hid_hi"], 1)
                    if age == 0 and j == 2:
                        exps(1, E1)
                if has_next:
                    split_w1(layer, p + 2, k, pair + 1, True)
                if has_up:
                    split_w2(layer, p, k, pair, age > 1)

            periods(act, E1, period1)

        @block.gpsimd
        def _(pool):
            pool.memset(eps_t[:], EPS).then_inc(cleared, 1)
            pool.memset(hpi_t[:], PI / 2).then_inc(cleared, 1)
            pool.memset(h[:], 0.0).then_inc(cleared, 1)
            pool.memset(mv[:], 1.0).then_inc(cleared, 1)
            pool.memset(gl[:], 0.0).then_inc(cleared, 1)
            pool.memset(v_pad[:], 0.0).then_inc(cleared, 1)

            def low_w1(layer, e, k, pair, reused):
                s = layer["s"]
                if reused:
                    pool.wait_ge(s["up"], 6 * e - 6)
                for n, a in enumerate((0, W1C)):
                    pool.wait_ge(s["w1_hi"], 2 * e + n + 1)
                    pool.tensor_tensor(w1_lo[k][:, a:a + W1C], raw1[k][:, a:a + W1C], w1_hi[k][:, a:a + W1C].bitcast(F32),
                                       ALU.subtract).then_inc(s["w1_lo"], 1)

            def low_w2(layer, e, k, pair, reused):
                s, n = layer["s"], layer["W2"]
                if reused:
                    pool.wait_ge(s["down"], NTILES * e - NTILES)
                pool.wait_ge(s["w2_hi"], e + 1)
                pool.tensor_tensor(w2_lo[k][:, 0:n], raw2[k][:, 0:n], w2_hi[k][:, 0:n].bitcast(F32), ALU.subtract)\
                    .then_inc(s["w2_lo"], 1)

            def make_period(layer):
                def period(p, k, pair, age, has_up, has_next):
                    if has_next:
                        low_w1(layer, p + 2, k, pair + 1, True)
                    if has_up:
                        low_w2(layer, p, k, pair, age > 1)
                return period

            pool.wait_ge(pk1_in, 16)
            pool.wait_ge(ln[0]["xn"], NTILES)
            for i, r in enumerate(ROWS):
                pool.tensor_tensor(h[0:r, i, :], h[0:r, i, :], p1("bp", r), ALU.add).then_inc(hb_ready, 1)
            low_w1(LAYERS[0], 0, 0, 0, False)
            low_w1(LAYERS[0], 1, 1, 0, False)
            pool.wait_ge(ln[1]["xn"], NTILES)
            for i, r in enumerate(ROWS):
                pool.tensor_tensor(h[0:r, i, :], h[0:r, i, :], xn[0:r, i, :], ALU.add).then_inc(hx_ready, 1)
            periods(pool, E0, make_period(LAYERS[0]))
            pool.wait_ge(tr[3]["mm"], NTILES)
            pool.memset(hz[:], 0.0).then_inc(hx_ready, 1)
            pool.wait_ge(ln[2]["xn"], NTILES)
            for i, r in enumerate(ROWS):
                pool.tensor_tensor(h[0:r, i, :], h[0:r, i, :], xn[0:r, i, :], ALU.add).then_inc(hx_ready, 1)
                pool.wait_ge(hx_ready, NTILES + 2 + i)
                pool.tensor_tensor(h[0:r, i, :], h[0:r, i, :], p2("beta", r), ALU.add).then_inc(base2_ready, 1)
            pool.wait_ge(rot_step, DQ_STEP)
            pool.wait_ge(sin_ready, 2)
            pool.tensor_tensor(wq[:], dq[:], cos_h[:].unsqueeze(1).to_broadcast([128, 3, HALF]), ALU.mult)\
                .then_inc(wq_ready, 1)
            low_w1(LAYERS[1], 0, 0, 0, False)
            low_w1(LAYERS[1], 1, 1, 0, False)
            periods(pool, E1, make_period(LAYERS[1]))

        @block.vector
        def _(dve):
            def row_stats(k, src, ready):
                s = ln[k]
                for i, r in enumerate(ROWS):
                    ready(i)
                    dve.bn_stats(stats[0:r, i, :], src[0:r, i, :]).then_inc(s["step"], 1)
                for i, r in enumerate(ROWS):
                    dve.wait_ge(s["step"], i + 1)
                    dve.bn_aggr(mv[0:r, i, :], stats[0:r, i, :]).then_inc(s["mean"], 1)

            def layer_norm(k, src, ready):
                s = ln[k]
                row_stats(k, src, ready)
                dve.wait_ge(s["sd"], 1)
                dve.reciprocal(rstd[:], sd[:]).then_inc(s["step"], 1)
                dve.wait_ge(s["step"], NTILES + 1)
                for i, r in enumerate(ROWS):
                    dve.tensor_scalar(xn[0:r, i, :], src[0:r, i, :], mv[0:r, i, 0:1], rstd[0:r, i:i + 1], ALU.subtract,
                                      ALU.mult).then_inc(s["xn"], 1)

            def evac_transposed(k, b0, n=KB):
                dve.wait_ge(tr[k]["mm"], NTILES)
                dve.tensor_copy(xt[0:n, 1, 0:4 * TILE].rearrange("p (t c) -> p t c", t=4),
                                ps[0:n, b0 + 1, :].rearrange("p (t c) -> p t c", t=4)[:, :, 0:TILE]).then_inc(tr[k]["dve"], 1)

            def split_x(k):
                dve.wait_ge(xhi[k], 1)
                dve.tensor_tensor(xa_lo[:], xt[:, 0, :], xa_hi[:].bitcast(F32), ALU.subtract).then_inc(xlo[k], 1)
                dve.wait_ge(xhi[k], 2)
                dve.tensor_tensor(xb_hl[64:128, :], xt[64:128, 1, :], xb_hi[64:128, :].bitcast(F32), ALU.subtract)\
                   .then_inc(xlo[k], 1)

            def router(k, E, top, on_probs):
                s, n = rt[k], [0]

                def step(ins):
                    n[0] += 1
                    ins.then_inc(s["step"], 1)
                    dve.wait_ge(s["step"], n[0])

                g, x, c = gl[:, :, 0:E], gexp[:, :, 0:E], comb[:, :, 0:E]
                over = [128, NTILES, E]
                key = x if on_probs else g
                bound = top8[:, :, top - 1:top].to_broadcast(over)

                def each(v):
                    return v.unsqueeze(2).to_broadcast(over)

                def normalize(v):
                    step(dve.tensor_reduce(gsum[:], v, AX_X, ALU.add))
                    step(dve.reciprocal(grec[:], gsum[:]))

                def logits():
                    dve.wait_ge(s["mm"], NTILES)
                    bank = ps[:, 6, 0:NTILES * E].rearrange("p (t e) -> p t e", e=E)
                    for tiles, m in ((slice(0, 4), TILE), (slice(4, 5), ROWS[4])):
                        n[0] += 1
                        if k == 0:
                            dve.tensor_tensor(gl[0:m, tiles, 0:E], bank[0:m, tiles, :], p2("gb", m).unsqueeze(1)
                                              .to_broadcast([m, tiles.stop - tiles.start, E]), ALU.add).then_inc(s["step"], 1)
                        else:
                            dve.tensor_copy(gl[0:m, tiles, 0:E], bank[0:m, tiles, :]).then_inc(s["step"], 1)
                    dve.wait_ge(s["step"], n[0])
                    step(dve.tensor_reduce(gmax[:], g, AX_X, ALU.max))
                    dve.tensor_tensor(x, g, each(gmax[:]), ALU.subtract).then_inc(s["shift"], 1)

                def probs():
                    dve.wait_ge(s["exp"], 1)
                    normalize(x)
                    step(dve.tensor_tensor(x, x, each(grec[:]), ALU.mult))

                def largest():
                    for i in range(NTILES):
                        dve.max(top8[:, i, :], key[:, i, :]).then_inc(s["step"], 1)
                        n[0] += 1
                    dve.wait_ge(s["step"], n[0])
                    dve.tensor_tensor(same[0][:, :, 0:E], key, bound, ALU.is_equal).then_inc(s["step"], 1)
                    dve.tensor_tensor(equal[:, :, 0:E], key, bound, ALU.is_equal).then_inc(s["step"], 1)
                    n[0] += 2
                    step(dve.tensor_tensor(above[:, :, 0:E], key, bound, ALU.is_gt))
                    step(dve.tensor_reduce(count[:], above[:, :, 0:E], AX_X, ALU.add))

                def places(d0, d1):
                    d = d0
                    while d < d1:
                        turn = (d.bit_length() - 1) % 2
                        a, b = same[turn], same[1 - turn]
                        dve.tensor_copy(b[:, :, 0:d], a[:, :, 0:d]).then_inc(s["step"], 1)
                        n[0] += 1
                        step(dve.tensor_tensor(b[:, :, d:E], a[:, :, d:E], a[:, :, 0:E - d], ALU.add))
                        d *= 2

                def weights():
                    place = same[(E.bit_length() - 1) % 2][:, :, 0:E]
                    step(dve.tensor_tensor(place, place, each(count[:]), ALU.add))
                    step(dve.scalar_tensor_tensor(place, place, float(top), equal[:, :, 0:E], ALU.is_le, ALU.mult))
                    step(dve.tensor_tensor(place, place, above[:, :, 0:E], ALU.add))
                    if not on_probs:
                        dve.wait_ge(s["exp"], 1)
                    last = dve.tensor_tensor(c, place, x, ALU.mult)
                    if not on_probs:
                        step(last)
                        normalize(c)
                        last = dve.tensor_tensor(c, c, each(grec[:]), ALU.mult)
                    last.then_inc(s["comb"], 1)

                return logits, probs, largest, places, weights

            dve.memset(prob[96:128], 1.0).then_inc(cleared, 1)
            dve.wait_ge(cleared, CLEARED)

            def embedded(i):
                r = ROWS[i]
                dve.wait_ge(tok_mm, i + 1)
                dve.tensor_tensor(h[0:r, i, :], ps[0:r, i, 0:DIM], tokw_sb[0:r, PIXC, :], ALU.add).then_inc(h0_ready, 1)
                dve.wait_ge(h0_ready, i + 1)

            layer_norm(0, h, embedded)
            evac_transposed(0, 5)

            dve.wait_ge(pk1_in, 16)
            for c in range(2):
                dve.wait_ge(qk_mm, 2 * c + 1)
                dve.tensor_scalar(q_sb[0:HD, c, :].rearrange("p (a b) -> p a b", a=2), ps[0:HD, 4 * c:4 * c + 2, 0:HALF],
                                  p1("bqk")[0:HD, c:c + 1], HDIM ** -0.5, ALU.add, ALU.mult).then_inc(q_ready, 1)
            for c in range(2):
                dve.wait_ge(q_ready, c + 1)
                for g in range(HG):
                    dve.tensor_scalar(qd[0:HD, c, :, g * SEQ:(g + 1) * SEQ], q_sb[0:HD, c, :].rearrange("p (b n) -> p b n", n=SEQ),
                                      p1("head")[0:HD, g:g + 1], None, ALU.mult).then_inc(qd_ready, 1)
            delta = p1("delta", HROWS).unsqueeze(1).to_broadcast([HROWS, 2 * HEADS, SEQ])
            for mix, name, ready in ((lmix, "wl", lmix_ready), (wmix, "ww", wmix_ready)):
                dve.tensor_tensor(mix[0:HROWS].rearrange("p a g n -> p (a g) n"),
                                  p1(name, HROWS).unsqueeze(2).to_broadcast([HROWS, 2 * HEADS, SEQ]), delta, ALU.mult)\
                   .then_inc(ready, 1)

            by_image = [HROWS, IMAGES // 2, SEQ]

            def shift(n):
                at = QUARTERS[n]
                x = lg[0:HROWS, at, :].rearrange("p (b m) -> p b m", m=SEQ)
                dve.wait_ge(lg_ready, n + 1)
                dve.tensor_reduce(smax[0:HROWS, at, :], x, AX_X, ALU.max).then_inc(smax_ready, 1)
                dve.wait_ge(smax_ready, n + 1)
                dve.tensor_tensor(x, x, smax[0:HROWS, at, :].unsqueeze(2).to_broadcast(by_image), ALU.subtract)\
                   .then_inc(lg_shift, 1)

            def normalize_probs(n):
                at = QUARTERS[n]
                y = prob[0:HROWS, at, :].rearrange("p (b m) -> p b m", m=SEQ)
                dve.wait_ge(exp_ready, n + 1)
                dve.tensor_reduce(ssum[0:HROWS, at, :], y, AX_X, ALU.add).then_inc(ssum_ready, 1)
                dve.wait_ge(ssum_ready, n + 1)
                dve.reciprocal(srec[0:HROWS, at, :], ssum[0:HROWS, at, :]).then_inc(srec_ready, 1)
                dve.wait_ge(srec_ready, n + 1)
                dve.tensor_tensor(y, y, srec[0:HROWS, at, :].unsqueeze(2).to_broadcast(by_image), ALU.mult)\
                   .then_inc(prob_ready, 1)

            shift(0)
            shift(1)
            normalize_probs(0)
            normalize_probs(1)
            shift(2)
            shift(3)
            normalize_probs(2)
            normalize_probs(3)

            for i, r in enumerate(ROWS):
                dve.wait_ge(mix_mm, i + 1)
                if i >= 2:
                    dve.wait_ge(tr[1]["mm"], i - 1)
                ni = TILE_IMGS[i]
                by = [r, HEADS, ni, SEQ]
                dve.tensor_tensor(abd[i % 2][0:r, :, 0:r].rearrange("p g (b n) -> p g b n", n=SEQ),
                                  ps[0:r, 4 + i % 2, 0:HEADS * SEQ].rearrange("p (g n) -> p g n", n=SEQ).unsqueeze(2)
                                  .to_broadcast(by),
                                  p1("mask", r)[:, 0:ni].unsqueeze(1).unsqueeze(3).to_broadcast(by), ALU.mult)\
                   .then_inc(abd_ready, 1)
            evac_transposed(1, 0)
            def attended(i):
                r = ROWS[i]
                dve.wait_ge(proj_mm, i + 1)
                dve.wait_ge(hb_ready, i + 1)
                dve.tensor_tensor(h[0:r, i, :], ps[0:r, 3 + i, 0:DIM], h[0:r, i, :], ALU.add).then_inc(h1_ready, 1)
                dve.wait_ge(h1_ready, i + 1)

            row_stats(1, h, attended)
            dve.wait_ge(ln[1]["mean"], NTILES)
            dve.tensor_copy(squares[:, 0, :], mv[:, :, 1]).then_inc(ssq_ready, 1)
            dve.tensor_scalar(squares[:, 1, :], mv[:, :, 1], EPS, None, ALU.add).then_inc(ssq_ready, 1)
            dve.wait_ge(ssq_ready, 2)
            dve.reciprocal(squares[:, 1, :], squares[:, 1, :]).then_inc(ssq_ready, 1)
            dve.wait_ge(ssq_ready, 3)
            dve.tensor_tensor(squares[:, 1, :], squares[:, 1, :], mv[:, :, 1], ALU.mult).then_inc(ssq_ready, 1)
            dve.wait_ge(rms_sd, 1)
            dve.reciprocal(rroots[:], roots[:]).then_inc(rms_rs, 1)
            dve.wait_ge(rms_rs, 1)
            for i, r in enumerate(ROWS):
                dve.tensor_scalar(xn[0:r, i, :], h[0:r, i, :], mv[0:r, i, 0:1], rroots[0:r, 0, i:i + 1], ALU.subtract,
                                  ALU.mult).then_inc(ln[1]["xn"], 1)
            dve.wait_ge(pk2_in, 16)
            for i, r in enumerate(ROWS):
                dve.wait_ge(ln[1]["xn"], i + 1)
                dve.scalar_tensor_tensor(xw[0:r, i, :], xn[0:r, i, :], rroots[0:r, 1, i:i + 1], p2("scale", r), ALU.mult,
                                         ALU.mult)\
                   .then_inc(t_ready, 1)
            b1v = b1x[:].rearrange("p (e j) -> p e j", j=6)
            p2b = p2("b1").rearrange("p (e j) -> p e j", j=6)
            dve.tensor_copy(b1v[:, :, 0:C0], p2b[:, :, 0:C0]).then_inc(b1_ready, 1)
            dve.tensor_scalar(b1v[:, :, C0:6], p2b[:, :, C0:6], 1.0, None, ALU.add).then_inc(b1_ready, 1)
            evac_transposed(2, 0, 128)
            split_x(0)

            def add_expert(s, p, k, i, age):
                r = ROWS[i]
                dve.wait_ge(s["down"], NTILES * p - NTILES + i + 1)
                if age > 1 or i:
                    dve.wait_ge(s["y"], NTILES * p - NTILES + i)
                dve.scalar_tensor_tensor(h[0:r, i, :], ps[0:r, DOWN_BANKS[i], 0:DIM], comb[0:r, i, bass.ds(p - 1, 1)],
                                         h[0:r, i, :], ALU.mult, ALU.add).then_inc(s["y"], 1)

            def bias_rows():
                dve.wait_ge(moe[0]["y"], NTILES * (E0 - 1))
                for i, r in enumerate(ROWS):
                    dve.wait_ge(b2_mm, i + 1)
                    dve.tensor_tensor(h[0:r, i, :], ps[0:r, BIAS_BANKS[i], 0:DIM], h[0:r, i, :], ALU.add)\
                       .then_inc(base_ready, 1)
                dve.wait_ge(base_ready, NTILES)

            logits, probs, largest, places, weights = router(0, E0, TOPK, False)

            def period0(p, k, pair, age, has_up, has_next):
                s = moe[0]

                def gate(j):
                    dve.wait_ge(s["up"], 6 * p + 2 * j + 1)
                    if age:
                        dve.wait_ge(s["gact"], C0 * p - C0 + j + 1)
                    slot = 2 * ((2 * j) % 3)
                    dve.tensor_scalar(glu[:, j, :].rearrange("p (a b) -> p a b", a=2), ps[:, slot:slot + 2, 0:HALF],
                                      b1x[:, bass.ds(6 * p + j, 1)], LIMIT, ALU.add, ALU.min).then_inc(s["glu"], 1)

                def clamp(j):
                    dve.wait_ge(s["lin"], C0 * p + j + 1)
                    dve.tensor_scalar(lin[:, j, :], lin[:, j, :], 1.0 + LIMIT, 1.0 - LIMIT, ALU.min, ALU.max)\
                       .then_inc(s["clamp"], 1)

                def value(j):
                    dve.wait_ge(s["clamp"], C0 * p + j + 1)
                    dve.wait_ge(s["gact"], C0 * p + j + 1)
                    if age:
                        dve.wait_ge(s["hid_lo"], C0 * p - C0 + j + 1)
                    dve.tensor_tensor(aval[:, j, :], gact[:, j, :], lin[:, j, :], ALU.mult).then_inc(s["aval"], 1)

                def low(j, e, b):
                    dve.wait_ge(s["hid_hi"], C0 * e + j + 1)
                    if age > 1 and j == 0:
                        dve.wait_ge(s["down"], NTILES * p - NTILES)
                    dve.tensor_tensor(hid_lo[b][:, j, :], aval[:, j, :], hid_hi[b][:, j, :].bitcast(F32), ALU.subtract)\
                       .then_inc(s["hid_lo"], 1)

                def add(i):
                    if age == 1:
                        dve.wait_ge(hx_ready, i + 1)
                    if age:
                        add_expert(s, p, k, i, age)

                if age:
                    low(2, p - 1, 1 - k)
                if has_up:
                    gate(0)
                    clamp(0)
                    gate(1)
                    value(0)
                    clamp(1)
                    if age == 1:
                        places(1, E0)
                    gate(2)
                    low(0, p, k)
                    value(1)
                if not has_up:
                    bias_rows()
                if age == 1:
                    weights()
                    dve.wait_ge(rt[0]["comb"], 1)
                add(0)
                if has_up:
                    clamp(2)
                add(1)
                if has_up:
                    low(1, p, k)
                add(2)
                if has_up:
                    value(2)
                add(3)
                add(4)

            logits()
            largest()
            dve.wait_ge(b1_ready, 2)
            periods(dve, E0, period0)

            layer_norm(2, h, lambda i: dve.wait_ge(moe[0]["y"], NTILES * (E0 - 1) + i + 1))
            evac_transposed(3, 5)
            n = [0]

            def part(ins):
                n[0] += 1
                ins.then_inc(rot_step, 1)

            def step(ins):
                part(ins)
                dve.wait_ge(rot_step, n[0])

            part(dve.memset(hs[:, :, 3, :], 1.0))
            for c in range(3):
                bank, a = 2 * (c // 2) + 1, 64 * (c % 2)
                dve.wait_ge(wall_mm, bank + 1)
                dve.tensor_scalar(bvec[64:128, c, :], ps[a:a + 64, bank, 0:HALF], p2("ball")[a:a + 64, c:c + 1], None,
                                  ALU.add).then_inc(bvec_ready, 1)
            dve.wait_ge(bvec_ready, 6)
            step(dve.tensor_tensor(bsq[:], bvec[:], bvec[:], ALU.mult))
            step(dve.tensor_tensor(norm[:], bsq[:, 0, :], bsq[:, 1, :], ALU.add))
            dve.tensor_tensor(norm[:], norm[:], bsq[:, 2, :], ALU.add).then_inc(nsq_ready, 1)
            dve.wait_ge(norm_ready, 1)
            step(dve.tensor_scalar(norm[:], norm[:], 1e-8, None, ALU.max))
            part(dve.tensor_scalar(turns[:], norm[:], 0.25 / PI, MAGIC, ALU.mult, ALU.add))
            step(dve.tensor_scalar(half_ang[:], norm[:], 0.5, None, ALU.mult))
            step(dve.tensor_scalar(turns[:], turns[:], MAGIC, None, ALU.subtract))
            step(dve.scalar_tensor_tensor(half_ang[:], turns[:], -TWO_PI_HI, half_ang[:], ALU.mult, ALU.add))
            step(dve.scalar_tensor_tensor(half_ang[:], turns[:], -TWO_PI_LO, half_ang[:], ALU.mult, ALU.add))
            dve.tensor_scalar(half_ang[:], half_ang[:], 3.1415925, -3.1415925, ALU.min, ALU.max).then_inc(ang_ready, 1)
            dve.wait_ge(ang_ready, 1)
            dve.scalar_tensor_tensor(habs[:], half_ang[:], -1.0, half_ang[:], ALU.mult, ALU.max).then_inc(ang_ready, 1)
            step(dve.reciprocal(rnorm[:], norm[:]))
            part(dve.tensor_tensor(bun[:, 0, :], bvec[:, 2, :], rnorm[:], ALU.mult))
            part(dve.scalar_tensor_tensor(bun[:, 1, :], bvec[:, 1, :], -1.0, rnorm[:], ALU.mult, ALU.mult))
            step(dve.tensor_tensor(bun[:, 2, :], bvec[:, 0, :], rnorm[:], ALU.mult))
            by = [128, 3, HALF]
            dve.wait_ge(dec_ready, 2)
            d2 = dec[:].unsqueeze(1).to_broadcast(by)
            dve.wait_ge(sin_ready, 1)
            step(dve.tensor_tensor(qv[:], bun[:], sin_h[:].unsqueeze(1).to_broadcast(by), ALU.mult))
            step(dve.scalar_tensor_tensor(dq[:], qv[:], 2.0, d2, ALU.mult, ALU.mult))
            assert n[0] == DQ_STEP
            part(dve.tensor_tensor(qq[:], dq[:], qv[:], ALU.mult))
            part(dve.tensor_tensor(qx[:, 0:2, :], dq[:, 0:2, :], qv[:, 1:3, :], ALU.mult))
            part(dve.tensor_tensor(qx[:, 2, :], dq[:, 0, :], qv[:, 2, :], ALU.mult))
            dve.wait_ge(rot_step, DQ_STEP + 1)
            step(dve.tensor_tensor(bsq[:], d2, qq[:], ALU.subtract))

            def entry(o, c):
                return rmat[:, :, o, c, :].rearrange("p t b -> p b t")

            def by_image(ap):
                return ap.rearrange("p (b t) -> p b t", t=SEQ)

            for o, (a, b) in enumerate(((1, 2), (2, 0), (0, 1))):
                part(dve.tensor_tensor(entry(o, o), by_image(bsq[:, a, :]), by_image(qq[:, b, :]), ALU.subtract))
            dve.wait_ge(wq_ready, 1)
            for o, c, pair, w, op in ((0, 1, 0, 2, ALU.subtract), (0, 2, 2, 1, ALU.add), (1, 0, 0, 2, ALU.add),
                                      (1, 2, 1, 0, ALU.subtract), (2, 0, 2, 1, ALU.subtract), (2, 1, 1, 0, ALU.add)):
                part(dve.tensor_tensor(entry(o, c), by_image(qx[:, pair, :]), by_image(wq[:, w, :]), op))
            dve.wait_ge(inj_ready, 5)
            step(dve.tensor_copy(hs[:, 0, 0:3, :], rmat[:, 0, :, 3, :]))
            QI = IMAGES // 4
            for t in range(1, SEQ):
                for chain in range(2):
                    im = slice(chain * QI, (chain + 1) * QI)
                    if t > 1:
                        dve.wait_ge(scan_step[chain], 2 * t - 2)
                    dve.tensor_tensor(prod[:, :, :, im], rmat[:, t, :, :, im], hs[:, t - 1, :, im].unsqueeze(1)
                                      .to_broadcast([128, 3, 4, QI]), ALU.mult).then_inc(scan_step[chain], 1)
                for chain in range(2):
                    im = slice(chain * QI, (chain + 1) * QI)
                    dve.wait_ge(scan_step[chain], 2 * t - 1)
                    dve.tensor_reduce(hs[:, t, 0:3, im], prod[:, :, :, im].rearrange("p o c b -> p o b c"), AX_X, ALU.add)\
                       .then_inc(scan_step[chain], 1)
            for chain in range(2):
                dve.wait_ge(scan_step[chain], 2 * SEQ - 2)
            dve.wait_ge(hx_ready, NTILES + 1)
            for c in range(3):
                dve.tensor_copy(by_image(hz[64:128, c, HALF:TOKENS]), hs[64:128, :, c, :].rearrange("p t b -> p b t"))\
                   .then_inc(hz_dve, 1)
            row_stats(3, xw, lambda i: dve.wait_ge(ht_ready, i + 1))
            for i, r in enumerate(ROWS):
                dve.wait_ge(ln[3]["mean"], i + 1)
                dve.scalar_tensor_tensor(xw[0:r, i, :], xw[0:r, i, :], mv[0:r, i, 0:1], p2("gamma", r), ALU.subtract,
                                         ALU.mult).then_inc(t_ready, 1)
            dve.wait_ge(ln[3]["sd"], 1)
            dve.reciprocal(rstd[:], sd[:]).then_inc(ln[3]["step"], 1)
            dve.wait_ge(ln[3]["step"], NTILES + 1)
            dve.wait_ge(base2_ready, NTILES)
            for i, r in enumerate(ROWS):
                dve.wait_ge(t_ready, NTILES + i + 1)
                dve.scalar_tensor_tensor(h[0:r, i, :], xw[0:r, i, :], rstd[0:r, i:i + 1], h[0:r, i, :], ALU.mult, ALU.add)\
                   .then_inc(h3_ready, 1)
            layer_norm(4, h, lambda i: dve.wait_ge(h3_ready, i + 1))
            evac_transposed(4, 5, 128)
            split_x(1)
            logits, probs, largest, places, weights = router(1, E1, 1, True)

            def period1(p, k, pair, age, has_up, has_next):
                s = moe[1]
                for j in range(C1):
                    if has_up:
                        dve.wait_ge(s["hid_hi"], C1 * p + j + 1)
                        if j == 0 and age > 1:
                            dve.wait_ge(s["down"], NTILES * p - NTILES)
                        slot = 2 * (j % 3)
                        dve.scalar_tensor_tensor(hid_lo[k][:, j, :].rearrange("p (a b) -> p a b", a=2),
                                                 ps[:, slot:slot + 2, 0:HALF], 0.0,
                                                 hid_hi[k][:, j, :].bitcast(F32).rearrange("p (a b) -> p a b", a=2),
                                                 ALU.max, ALU.subtract).then_inc(s["hid_lo"], 1)
                        if age == 0 and j == 1:
                            logits()
                        elif age == 0 and j == 3:
                            probs()
                        elif age == 0 and j == 5:
                            largest()
                        elif age == 1 and j == 2:
                            places(1, E1)
                        elif age == 1 and j == 5:
                            weights()
                            dve.wait_ge(rt[1]["comb"], 1)
                if age:
                    for i in range(NTILES):
                        add_expert(s, p, k, i, age)

            periods(dve, E1, period1)

        @block.tensor
        def _(pe):
            def transposes(k, src, ready, b0, twice):
                for i, r in enumerate(ROWS):
                    ready(i)
                    b, c = (b0, 128 * i) if i < 4 else (b0 + 2, 0)
                    pe.transpose(ps[:, b, c:c + r], src[0:r, i, 0:128], ident[0:r, 0:r])
                    b, c = (b0 + 1, 128 * i) if i < 4 else (b0 + 2, 128)
                    ins = pe.transpose(ps[0:KB, b, c:c + r], src[0:r, i, 128:DIM], ident[0:r, 0:r])
                    if twice:
                        ins = pe.matmul(ps[KB:128, b, c:c + r], src[0:r, i, 128:DIM], ident[0:r, 0:r], start=True,
                                        stop=True, skip_group_check=True)
                    ins.then_inc(tr[k]["mm"], 1)

            def xt_ready(k):
                pe.wait_ge(tr[k]["act"], 3)
                pe.wait_ge(tr[k]["dve"], 1)

            def group(dst, pairs):
                for n, (a, b) in enumerate(pairs):
                    ins = pe.matmul(dst, a, b, start=(n == 0), stop=(n == len(pairs) - 1), skip_group_check=True)
                return ins

            pe.wait_ge(tokw_in, 16)
            for i, r in enumerate(ROWS):
                pe.wait_ge(xp_in[i], 16)
                a = PIXC * TILE * i
                group(ps[0:r, i, 0:DIM], [(xp_sb[:, a + c * r:a + (c + 1) * r], tokw_sb[:, c, :]) for c in range(PIXC)])\
                    .then_inc(tok_mm, 1)
            pe.wait_ge(ident_in, 16)
            transposes(0, xn, lambda i: pe.wait_ge(ln[0]["xn"], i + 1), 5, False)

            xt_ready(0)
            pe.wait_ge(pk1_in, 16)
            for n, (c, which) in enumerate(((0, 0), (0, 1), (1, 0), (1, 1))):
                w0_ = which * DIM + c * HD
                for kc, (name, kk) in enumerate((("wqkv_a", KA), ("wqkv_b", KB))):
                    for hh in range(2):
                        ins = pe.matmul(ps[0:HD, 2 * n + hh, 0:HALF], p1(name, kk)[:, w0_:w0_ + HD],
                                        xt[0:kk, kc, hh * HALF:(hh + 1) * HALF], start=(kc == 0), stop=(kc == 1),
                                        skip_group_check=True)
                ins.then_inc(qk_mm, 1)
            pe.wait_ge(rows_in, 16)
            for i, r in enumerate(ROWS):
                pe.wait_ge(q_ready, (1, 1, 1, 1, 2)[i])
                pe.wait_ge(k_ready, (0, 0, 1, 1, 1)[i]) if i >= 2 else None
                group(ps[0:r, i, 0:DIM], [
                    (rw("ones")[:, 0:r], rw("bv")),
                    (xt[0:KA, 0, tile_cols(i)], p1("wqkv_a")[:, 2 * DIM:3 * DIM]),
                    (xt[0:KB, 1, tile_cols(i)], p1("wqkv_b", KB)[:, 2 * DIM:3 * DIM])]).then_inc(v_mm, 1)
            pe.wait_ge(v_ready, NTILES)
            pe.wait_ge(k_ready, 2)

            def scores(n):
                hf, ih = QUARTERS[n] // 2, QUARTERS[n] % 2
                pe.wait_ge(qd_ready, (hf + 1) * HG)
                for b in range(IMAGES // 2):
                    img = ih * (IMAGES // 2) + b
                    ins = pe.matmul(ps[0:HROWS, QUARTERS[n], b * SEQ:(b + 1) * SEQ], qd[0:HD, hf, img, :],
                                    k_sb[0:HD, hf, img * SEQ:(img + 1) * SEQ], start=True, stop=True, skip_group_check=True)
                ins.then_inc(sc_mm, 1)

            def mix_scores(n):
                gh, ih = QUARTERS[n] // 2, QUARTERS[n] % 2
                pe.wait_ge(lmix_ready, 1)
                pe.wait_ge(sco_ready, 2 * ih + 2)
                group(ps[0:HROWS, 4 + QUARTERS[n], 0:HALF], [
                    (lmix[0:HROWS, hf, gh * HG:(gh + 1) * HG].rearrange("p g n -> p (g n)"), sco[0:HROWS, 2 * hf + ih, :])
                    for hf in range(2)]).then_inc(lg_mm, 1)

            scores(0)
            scores(1)
            scores(2)
            mix_scores(0)
            mix_scores(1)
            scores(3)
            mix_scores(2)
            mix_scores(3)
            pe.wait_ge(wmix_ready, 1)
            pe.wait_ge(bw_in, 16)
            pe.wait_ge(cleared, CLEARED)
            pe.wait_ge(v_ready, NTILES)

            def mix(i):
                r = ROWS[i]
                pe.wait_ge(prob_ready, 4)
                if i >= 2:
                    pe.wait_ge(abd_ready, i - 1)
                pairs = []
                for hf, K in ((0, HROWS + 1), (1, HROWS)):
                    both = prob[0:K, 2 * hf:2 * hf + 2, :].rearrange("p a b -> p (a b)")
                    pairs.append((both[:, tile_cols(i)], wmix[0:K, hf].rearrange("p g n -> p (g n)")))
                group(ps[0:r, 4 + i % 2, 0:HEADS * SEQ], pairs).then_inc(mix_mm, 1)

            def attend(i):
                r = ROWS[i]
                pe.wait_ge(abd_ready, i + 1)
                for q in range(HEADS // 2):
                    at = 32 * (q % 4)
                    b, c = (q // 4, 128 * i) if i < 4 else (2, 128 * (q // 4))
                    ins = group(ps[at:at + 32, b, c:c + r],
                                [(v_pad[0:r, i, g, :], abd[i % 2][0:r, g, 0:r]) for g in (2 * q, 2 * q + 1)])
                ins.then_inc(tr[1]["mm"], 1)

            mix(0)
            for i in range(NTILES):
                if i + 1 < NTILES:
                    mix(i + 1)
                attend(i)
            xt_ready(1)
            for i, r in enumerate(ROWS):
                group(ps[0:r, 3 + i, 0:DIM], [
                    (xt[0:KA, 0, tile_cols(i)], p1("wp_a")),
                    (xt[0:KB, 1, tile_cols(i)], p1("wp_b", KB))]).then_inc(proj_mm, 1)

            transposes(2, xw, lambda i: pe.wait_ge(t_ready, i + 1), 0, True)
            xt_ready(2)
            pe.wait_ge(pk2_in, 16)
            pe.wait_ge(h1_ready, NTILES)
            for i, r in enumerate(ROWS):
                group(ps[0:r, 6, i * E0:(i + 1) * E0], [
                    (xt[0:KA, 0, tile_cols(i)], p2("gate_a")),
                    (xt[0:KB, 1, tile_cols(i)], p2("gate_b", KB))]).then_inc(rt[0]["mm"], 1)

            def up(layer, p, k, age):
                s = layer["s"]
                pe.wait_ge(s["w1_hi"], 2 * p + 2)
                pe.wait_ge(s["w1_lo"], 2 * p + 2)
                hi, lo, first = w1_hi[k], w1_lo[k], age == 0
                for j in range(6):
                    if age > 1 and j < 2:
                        pe.wait_ge(s["y"], NTILES * p - 2 * NTILES + 2 + j)
                    if layer is LAYERS[0]:
                        col = (j // 2 + C0 * (j % 2)) * 128
                        if j in (1, 3, 5) and not (first and j < 3):
                            pe.wait_ge(s["glu"], C0 * p + (0, 1, 2)[j // 2])
                        elif j in (0, 2, 4) and not (first and j < 3):
                            pe.wait_ge(s["lin"], C0 * p + (-1, 0, 1)[j // 2])
                    else:
                        col = j * 128
                        if not (first and j < 3):
                            pe.wait_ge(s["hid_lo"], C1 * p + j - 2)
                    slot = 2 * (j % 3)
                    a, b = slice(col, col + 128), slice(W1C + col, W1C + col + 128)
                    parts = [(hi[:, a], xa_hi[:]), (hi[:, b], xb_hl[:]), (hi[:, a], xa_lo[:]), (lo[:, a], xa_hi[:]),
                             (lo[0:KB, b], xb_hl[0:KB, :])]
                    for n, (w, x) in enumerate(parts):
                        for hh in range(2):
                            ins = pe.matmul(ps[:, slot + hh, 0:HALF], w, x[:, hh * HALF:(hh + 1) * HALF], start=(n == 0),
                                            stop=(n == len(parts) - 1), skip_group_check=True)
                    ins.then_inc(s["up"], 1)

            def down(layer, p, k, age, has_up):
                s, C, b = layer["s"], layer["C"], 1 - k
                pe.wait_ge(s["hid_lo"], C * p)
                pe.wait_ge(s["w2_hi"], p)
                pe.wait_ge(s["w2_lo"], p)
                for i, r in enumerate(ROWS):
                    if i in (0, 2) and has_up:
                        if layer is LAYERS[0]:
                            pe.wait_ge(s["glu" if i else "lin"], C0 * p + (C0 if i else 2))
                        else:
                            pe.wait_ge(s["hid_lo"], C1 * p + (5 if i else 4))
                    elif age > 1 and (i > 2 or not has_up):
                        pe.wait_ge(s["y"], NTILES * p - 2 * NTILES + i + 1)
                    pairs = []
                    for c in range(C):
                        w = slice(c * DIM, (c + 1) * DIM)
                        pairs += [(hid_hi[b][:, c, tile_cols(i)], w2_hi[b][:, w]), (hid_hi[b][:, c, tile_cols(i)], w2_lo[b][:, w]),
                                  (hid_lo[b][:, c, tile_cols(i)], w2_hi[b][:, w])]
                    group(ps[0:r, DOWN_BANKS[i], 0:DIM], pairs).then_inc(s["down"], 1)

            def x_split(k):
                pe.wait_ge(xhi[k], 3)
                pe.wait_ge(xlo[k], 2)

            def make_period(layer, routing, last_work):
                def period(p, k, pair, age, has_up, has_next):
                    if has_up:
                        up(layer, p, k, age)
                    else:
                        last_work()
                    if age == 1:
                        pe.wait_ge(routing["shift"], 1)
                    if age:
                        down(layer, p, k, age, has_up)
                return period

            def bias_rows():
                pe.wait_ge(rt[0]["comb"], 1)
                pe.wait_ge(moe[0]["glu"], C0 * E0)
                pe.wait_ge(moe[0]["lin"], C0 * E0)
                for i, r in enumerate(ROWS):
                    b, c = (3, 128 * i) if i < 4 else (4, 0)
                    pe.transpose(ps[0:E0, b, c:c + r], comb[0:r, i, :], ident[0:r, 0:r]).then_inc(ct_mm, 1)
                pe.wait_ge(ct_ready, 2)
                for i, r in enumerate(ROWS):
                    if i >= 3:
                        pe.wait_ge(base_ready, i - 2)
                    pe.matmul(ps[0:r, BIAS_BANKS[i], 0:DIM], comb_t[:, i, 0:r], rw("b2", E0), start=True, stop=True)\
                      .then_inc(b2_mm, 1)

            x_split(0)
            periods(pe, E0, make_period(LAYERS[0], rt[0], bias_rows))

            transposes(3, xn, lambda i: pe.wait_ge(ln[2]["xn"], i + 1), 5, False)
            xt_ready(3)
            for n in range(4):
                for hh in range(2):
                    w = slice(2 * n * NBLK, min(2 * n + 2, 7) * NBLK)
                    at = ps[0:128, 2 * n + hh, 0:HALF] if n < 3 else ps[hh * 64:(hh + 1) * 64, 6, 0:HALF]
                    group(at, [(p2(name, kk)[:, w], xt[0:kk, kc, hh * HALF:(hh + 1) * HALF])
                               for kc, (name, kk) in enumerate((("wall_a", KA), ("wall_b", KB)))]).then_inc(wall_mm, 1)
            pe.wait_ge(hz_act, 3)
            pe.wait_ge(hz_dve, 3)
            pe.wait_ge(hx_ready, NTILES + 1)
            pe.wait_ge(inj_ready, 5)
            for i, r in enumerate(ROWS):
                a, b = tile_cols(i).start, tile_cols(i).stop
                for c in range(3):
                    at = ps[0:r, i, c * NBLK:(c + 1) * NBLK]
                    if b <= HALF:
                        ins = pe.transpose(at, hz[0:64, c, a:b], ident[0:64, 0:64])
                    elif a >= HALF:
                        ins = pe.transpose(at, hz[64:128, c, a:b], ident[64:128, 64:128])
                    else:
                        ins = pe.matmul(at, hz[:, c, a:b], p2("sel"), start=True, stop=True, skip_group_check=True)
                ins.then_inc(ht_mm, 1)
            transposes(4, xn, lambda i: pe.wait_ge(ln[4]["xn"], i + 1), 5, True)
            xt_ready(4)
            for i, r in enumerate(ROWS):
                group(ps[0:r, 6, i * E1:(i + 1) * E1], [
                    (xt[0:KA, 0, tile_cols(i)], p2("rout_a")),
                    (xt[0:KB, 1, tile_cols(i)], p2("rout_b", KB))]).then_inc(rt[1]["mm"], 1)
            x_split(1)

            periods(pe, E1, make_period(LAYERS[1], rt[1], lambda: None))


def lay_out(a):
    import numpy as np

    def ab(w):
        second = np.zeros((128, w.shape[1]), w.dtype)
        second[0:KB] = w[KA:DIM]
        return w[0:KA], second

    def every_row(v):
        return np.broadcast_to(v[None], (128, DIM))

    def pack(where, cols, parts, n=128):
        out = np.zeros((n, cols), np.float32)
        for name, (at, width) in where.items():
            p = parts[name]
            out[0:p.shape[0], at:at + width] = p
        return out

    x = a["x"].reshape(IMAGES, 3, 4, 16, 4, 16).transpose(1, 3, 5, 0, 2, 4).reshape(PIX, IMAGES, PATCHES)
    cols = np.zeros((PIX, IMAGES, SEQ), x.dtype)
    cols[:, :, 1:] = x
    cols = cols.reshape(PIXC, 128, TOKENS).transpose(1, 0, 2)
    xp = np.concatenate([cols[:, :, TILE * i:TILE * i + r].reshape(128, PIXC * r) for i, r in enumerate(ROWS)], axis=1)
    tokw = a["L0_tok_W"].T.reshape(PIXC, 128, DIM).transpose(1, 0, 2).reshape(128, PIXC * DIM)

    tokb = np.zeros((128, DIM), np.float32)
    tokb[0:TILE] = np.broadcast_to(a["L0_tok_b"], (TILE, DIM))
    tokb[0:TILE:SEQ] = a["cls_tok"].reshape(DIM)
    tokw = np.concatenate([tokw, tokb], axis=1)
    bqkv = a["L0_attn_b_qkv"]
    rows = pack(RW, RW_COLS, {
        "ones": np.ones((1, 128), np.float32), "bv": bqkv[None, 2 * DIM:],
        "bw": np.repeat(a["L0_attn_b_w"], SEQ)[None], "b2": a["L0_ffn_mlp2_b"]}, 16)

    wqkv_a, wqkv_b = ab(a["L0_attn_w_qkv"])
    wp_a, wp_b = ab(a["L0_attn_w_proj"])
    wl, ww = (np.repeat(a[name].reshape(2, HG, HEADS), SEQ, axis=1) for name in ("L0_attn_w_l", "L0_attn_w_w"))
    at = np.arange(HROWS)
    pk1 = pack(PK1, PK1_COLS, {
        "ident": np.eye(128, dtype=np.float32), "wqkv_a": wqkv_a, "wqkv_b": wqkv_b,
        "bqk": bqkv[0:2 * DIM].reshape(4, HD).T, "wl": np.concatenate([wl[0], wl[1]], axis=1),
        "head": (np.arange(HD)[:, None] // HDIM == np.arange(HG)).astype(np.float32),
        "bl": np.repeat(a["L0_attn_b_l"].reshape(2, HG), SEQ, axis=1).T, "ww": np.concatenate([ww[0], ww[1]], axis=1),
        "delta": (at[:, None] % SEQ == np.arange(SEQ)).astype(np.float32),
        "mask": (np.arange(TILE)[:, None] // SEQ == np.arange(IMG_TILE)).astype(np.float32),
        "wp_a": wp_a, "wp_b": wp_b, "bp": every_row(a["L0_attn_b_proj"])})

    def comps(w):
        return w.reshape(-1, NBLK, 3).transpose(0, 2, 1).reshape(-1, DIM)

    wall = np.concatenate([comps(a["L1_attn_Wb"]), np.repeat(a["L1_attn_Wd"], NBLK, axis=1), comps(a["L1_attn_Wi"])], axis=1)
    ball = np.concatenate([comps(a["L1_attn_bb"]), np.repeat(a["L1_attn_bd"], NBLK)[None], comps(a["L1_attn_bi"])], axis=1)
    ball = ball.reshape(7, NBLK).T
    wall_a, wall_b = ab(wall)
    gate_a, gate_b = ab(a["L0_ffn_gate_w"].T)
    rout_a, rout_b = ab(a["L1_ffn_router_w"])
    b1 = a["L0_ffn_mlp1_b"].reshape(E0, F0, 2).transpose(0, 2, 1).reshape(E0 * 6, 128).T

    pk2 = pack(PK2, PK2_COLS, {
        "scale": every_row(a["L0_ffn_norm_scale"]), "gamma": every_row(a["L1_attn_gamma"]), "beta": every_row(a["L1_attn_beta"]),
        "gate_a": gate_a, "gate_b": gate_b, "gb": np.broadcast_to(a["L0_ffn_gate_b"], (128, E0)), "b1": b1,
        "wall_a": wall_a, "wall_b": wall_b,
        "ball": np.concatenate([ball, ball]), "sel": np.concatenate([np.eye(NBLK, dtype=np.float32)] * 2),
        "rout_a": rout_a, "rout_b": rout_b})

    def expert_blocks(first, second):
        E, C = first.shape[0], second.shape[1] // 128
        tail = first[:, KA:DIM]
        second = second.reshape(E, C, 128, DIM).transpose(0, 2, 1, 3).reshape(E, 128, C * DIM)
        return np.concatenate([first[:, 0:KA], np.concatenate([tail, tail], axis=1), second], axis=2)

    m1 = a["L0_ffn_mlp1_w"].reshape(E0, F0, 2, DIM).transpose(0, 3, 2, 1).reshape(E0, DIM, 2 * F0)
    w0 = expert_blocks(m1, a["L0_ffn_mlp2_w"].transpose(0, 2, 1))
    w1 = expert_blocks(a["L1_ffn_wi"], a["L1_ffn_wo"])
    return {"xp": xp, "tokw": tokw, "rows": rows, "pk1": pk1, "pk2": pk2, "w0": w0, "w1": w1}


def kernel(**inputs):
    import numpy as np
    import concourse.bacc as bacc
    from concourse.bass_utils import run_bass_kernel_spmd

    nc = bacc.Bacc("TRN2", target_bir_lowering=False, num_devices=1)
    arrays, args = {}, []
    for name, v in lay_out({k: np.asarray(v) for k, v in inputs.items()}).items():
        v = np.ascontiguousarray(v)
        arrays[f"in_{name}"] = v
        args.append(nc.dram_tensor(f"in_{name}", v.shape, mybir.dt.from_np(v.dtype), kind="ExternalInput").ap())
    args.append(nc.dram_tensor("out_rows", (TOKENS, DIM), F32, kind="ExternalOutput").ap())
    build(nc, *args)
    r = run_bass_kernel_spmd(nc, [arrays], core_ids=[0])
    return r.results[0]["out_rows"].reshape(IMAGES, SEQ, DIM)
```
